# Optimizing a Trainium2 kernel written in Bass

```python
import numpy as np
import jax
import jax.numpy as jnp

def _softmax(x, axis=-1):
    return jax.nn.softmax(x, axis=axis)

def _gelu(x):
    return jax.nn.gelu(x, approximate=True)

def _silu(x):
    return jax.nn.silu(x)

def _sigmoid(x):
    return jax.nn.sigmoid(x)

def _layernorm(x, axis=-1, eps=1e-05):
    m = jnp.mean(x, axis=axis, keepdims=True)
    v = jnp.var(x, axis=axis, keepdims=True)
    return (x - m) / jnp.sqrt(v + eps)

def _scatter_add(tgt, idx, src, axis=0):
    return tgt.at[idx].add(src)

def _segment_sum(src, seg, n):
    return jax.ops.segment_sum(src, seg, n)
kernel_name = 'mk_adj_ffn_d1_adj_r2_b0ea98'

def setup_inputs(seed: int=0):
    np.random.seed(seed)
    _w = jnp.asarray

    def _rec_inputs():
        import jax
        import jax.numpy as jnp
        _gk = jax.random.key(seed)
        x = -0.0005207 + 1.001 * jax.random.normal(jax.random.fold_in(_gk, 1), (3327, 128), jnp.float32)
        _a = jax.random.bernoulli(jax.random.fold_in(_gk, 2), 0.00480914, (3327, 3327))
        _a = jnp.logical_or(_a, jnp.swapaxes(_a, -1, -2))
        _a = jnp.logical_or(_a, jnp.eye(3327, dtype=bool))
        adj = _a.astype(jnp.int32)
        return (x, adj)
    x, adj = _rec_inputs()

    def _L0_gnn_setup():
        import jax, jax.numpy as jnp
        import numpy as np
        N, D, H = (4096, 128, 128)
        KEEP_RATIO = 0.5
        TEMP = 1.0
        COS_EPS = 0.0001
        NEG = -9000000000000000.0

        def _cos_normalize(x):
            n = jnp.linalg.norm(x, axis=-1, keepdims=True)
            return x / jnp.maximum(n, COS_EPS)
        key = jax.random.key(seed)
        k1, k2, k3, k4 = jax.random.split(key, 4)
        features = jax.random.normal(k1, (N, D), dtype=jnp.float32)
        adj = jax.random.randint(k2, (N, N), 0, 2, dtype=jnp.int32)
        Wq = jax.random.normal(k3, (H, D), dtype=jnp.float32) * 0.001
        Wk = jax.random.normal(k4, (H, D), dtype=jnp.float32) * 0.001
        return {'features': features, 'adj': adj, 'Wq': Wq, 'Wk': Wk}
    _L0_gnn_all = _L0_gnn_setup()
    _L0_gnn_in = {k: v for k, v in _L0_gnn_all.items() if k in ('Wq', 'Wk')}
    del _L0_gnn_all

    def _L0_ffn_setup():
        import jax, jax.numpy as jnp
        import numpy as np
        D_IN, D_HID, D_OUT = (128, 256, 128)
        N_EXPERTS, TOP_K = (64, 2)
        B, S = (8, 2048)
        key = jax.random.key(seed)
        ks = jax.random.split(key, 8)
        scale_in = 1.0 / np.sqrt(D_IN)
        scale_hid = 1.0 / np.sqrt(D_HID)
        return {'x': jax.random.normal(ks[0], (B, S, D_IN), dtype=jnp.float32), 'Wr': jax.random.uniform(ks[1], (D_IN, N_EXPERTS), jnp.float32, -scale_in, scale_in), 'br': jax.random.uniform(ks[2], (N_EXPERTS,), jnp.float32, -scale_in, scale_in), 'W1': jax.random.uniform(ks[3], (N_EXPERTS, D_IN, D_HID), jnp.float32, -scale_in, scale_in), 'b1': jax.random.uniform(ks[4], (N_EXPERTS, D_HID), jnp.float32, -scale_in, scale_in), 'W2': jax.random.uniform(ks[5], (N_EXPERTS, D_HID, D_OUT), jnp.float32, -scale_hid, scale_hid), 'b2': jax.random.uniform(ks[6], (N_EXPERTS, D_OUT), jnp.float32, -scale_hid, scale_hid)}
    _L0_ffn_all = _L0_ffn_setup()
    _L0_ffn_in = {k: v for k, v in _L0_ffn_all.items() if k in ('Wr', 'br', 'W1', 'b1', 'W2', 'b2')}
    del _L0_ffn_all
    return {'x': x, 'adj': adj, 'L0_gnn_Wq': _L0_gnn_in['Wq'], 'L0_gnn_Wk': _L0_gnn_in['Wk'], 'L0_ffn_Wr': _L0_ffn_in['Wr'], 'L0_ffn_br': _L0_ffn_in['br'], 'L0_ffn_W1': _L0_ffn_in['W1'], 'L0_ffn_b1': _L0_ffn_in['b1'], 'L0_ffn_W2': _L0_ffn_in['W2'], 'L0_ffn_b2': _L0_ffn_in['b2']}

def reference(x, adj, L0_gnn_Wq, L0_gnn_Wk, L0_ffn_Wr, L0_ffn_br, L0_ffn_W1, L0_ffn_b1, L0_ffn_W2, L0_ffn_b2):
    import jax
    import jax.numpy as jnp

    def _L0_gnn_ref(features, adj, Wq, Wk):
        import jax, jax.numpy as jnp
        import numpy as np
        N, D, H = (4096, 128, 128)
        KEEP_RATIO = 0.5
        TEMP = 1.0
        COS_EPS = 0.0001
        NEG = -9000000000000000.0

        def _cos_normalize(x):
            n = jnp.linalg.norm(x, axis=-1, keepdims=True)
            return x / jnp.maximum(n, COS_EPS)
        Qn = _cos_normalize(features @ Wq.T)
        Kn = _cos_normalize(features @ Wk.T)
        raw_att = Kn @ Qn.T
        att = jnp.where(adj > 0, raw_att, NEG) * TEMP
        att = jax.nn.softmax(att, axis=1)
        prop_fea = att @ features
        adj_mask = (jnp.sum(adj, axis=1) > 0).astype(features.dtype)[:, None]
        prop_fea = adj_mask * prop_fea + (1.0 - adj_mask) * features
        return (1.0 - KEEP_RATIO) * prop_fea + KEEP_RATIO * features

    def _L0_ffn_ref(x, Wr, br, W1, b1, W2, b2):
        import jax, jax.numpy as jnp
        import numpy as np
        D_IN, D_HID, D_OUT = (128, 256, 128)
        N_EXPERTS, TOP_K = (64, 2)
        B, S = (8, 2048)
        Bx, Sx, D = x.shape
        xf = x.reshape(-1, D)
        T = xf.shape[0]
        E = Wr.shape[1]
        logits = xf @ Wr + br
        topk_logits, topk_idx = jax.lax.top_k(logits, TOP_K)
        gates = jax.nn.softmax(topk_logits, axis=1)
        combine = jnp.zeros((T, E), xf.dtype).at[jnp.arange(T)[:, None], topk_idx].add(gates)
        out = jnp.zeros((T, W2.shape[-1]), xf.dtype)
        for e in range(E):
            h = jax.nn.relu(xf @ W1[e] + b1[e])
            y = h @ W2[e] + b2[e]
            out = out + combine[:, e:e + 1] * y
        return out.reshape(Bx, Sx, -1)
    x = x + _L0_gnn_ref(_layernorm(x, axis=-1), adj, L0_gnn_Wq, L0_gnn_Wk)
    x = x + _L0_ffn_ref(_layernorm(x, axis=-1)[None], L0_ffn_Wr, L0_ffn_br, L0_ffn_W1, L0_ffn_b1, L0_ffn_W2, L0_ffn_b2)[0]
    return x

_drawn_inputs = setup_inputs


def setup_inputs(seed=0):
    import zlib

    import numpy as np

    out = dict(_drawn_inputs(seed))
    spreads = {}
    factors = {'L0_gnn_Wq': 5.166, 'L0_gnn_Wk': 4.959, 'L0_ffn_b1': 5.821, 'L0_ffn_b2': 3.371}
    for name, (base, spread) in spreads.items():
        noise = np.random.default_rng([zlib.crc32(name.encode()), seed]).standard_normal(out[name].shape)
        drawn = base * np.exp(spread * noise) if base else spread * noise
        out[name] = jnp.asarray(drawn.astype(out[name].dtype))
    for name, factor in factors.items():
        out[name] = (out[name] * factor).astype(out[name].dtype)
    return out
```

```python
import concourse.bass as bass
from concourse import mybir
from contextlib import ExitStack

N_TOK, D, HID, N_EXP = 3327, 128, 256, 64
P = 128
TILES = -(-N_TOK // P)
NPAD = TILES * P
BLOCKS = TILES // 2
PAIRS = TILES // 2
CAP = NPAD + P
FTILES = 116
SPARE = N_EXP * CAP
XS_ROWS = SPARE + FTILES * P
YT_ROWS = 2 * NPAD
NOWHERE = 1 << 20
EPS = 1e-5
W1C = HID + 2
FXC = 2 * D + 1
LOOP_LINKS = 34
BIG = 3 * NPAD * 2


def gnn_moe_program(nc, x_in, adj_in, wqk_in, wr_in, br_in, w1_in, w2_in, b2_in, out):
    fp32, bf16, fp16 = mybir.dt.float32, mybir.dt.bfloat16, mybir.dt.float16
    i32, u32 = mybir.dt.int32, mybir.dt.uint32
    ALU, ACT, AX = mybir.AluOpType, mybir.ActivationFunctionType, mybir.AxisListType
    ds = bass.ds

    assert (2 * N_TOK + N_EXP * (P - 1)) // P <= FTILES
    with ExitStack() as ctx:
        def sb(name, shape, dt):
            return ctx.enter_context(nc.sbuf_tensor(name, shape, dt))

        def sem(name):
            return ctx.enter_context(nc.semaphore(name))

        x_sb = sb("x_sb", [P, TILES, D], fp32)
        fx = sb("fx", [P, TILES, FXC], fp16)
        w1_sb = sb("w1_sb", [P, N_EXP * W1C], fp32)
        big = sb("big", [P, BIG], fp32)
        raw = big[:, 0:2 * NPAD].bitcast(i32).rearrange("p (s n) -> p s n", s=2)
        qk = big[:, 2 * NPAD:4 * NPAD].bitcast(fp16).rearrange("p (q n) -> p q n", q=4)
        mask = big[:, 4 * NPAD:6 * NPAD].bitcast(bf16).rearrange("p (s n) -> p s n", s=4)
        w2_sb = big[:, 0:N_EXP * HID]
        f32_sb = w1_sb[:, 0:NPAD].rearrange("p (t d) -> p t d", d=D)
        qk32 = w1_sb[:, NPAD:3 * NPAD].rearrange("p (t q h) -> p t q h", q=2, h=D)
        y_sb = [w1_sb[:, c * NPAD:(c + 1) * NPAD].rearrange("p (t d) -> p t d", d=D) for c in range(2)]
        p32 = sb("p32", [P, 3, 512], fp32)
        phi = sb("phi", [P, 3, 512], fp16)
        plo = sb("plo", [P, 3, 512], fp16)
        pay = sb("pay", [P, 2, 2, 2, D + 1], fp32)
        c_all = sb("c_all", [P, 2, 2, N_EXP], bf16)
        gates = sb("gates", [P, TILES, 2], fp32)
        id32 = sb("id32", [P, P], fp32)
        id16 = sb("id16", [P, P], fp16)
        idm = sb("idm", [P, P], bf16)
        tri = sb("tri", [P, P], bf16)
        ones = sb("ones", [P, P], bf16)
        wqk = sb("wqk", [P, 2 * D], fp32)
        wr = sb("wr", [P, N_EXP], fp32)
        br = sb("br", [P, N_EXP], fp32)
        b2 = sb("b2", [N_EXP, D], fp32)
        iota_e = sb("iota_e", [P, N_EXP], fp32)
        region = sb("region", [P, N_EXP], fp32)
        dest = sb("dest", [P, 2, TILES], i32)
        tok = sb("tok", [P, TILES], fp32)
        padx = sb("padx", [P, TILES], fp32)
        srow = sb("srow", [P, 1], fp32)
        spare = sb("spare", [P, 1], fp32)
        m_half = sb("m_half", [P, 2 * TILES], fp32)
        zero_e = sb("zero_e", [P, N_EXP], fp32)
        padrow = sb("padrow", [P, D + 1], fp32)
        stats = sb("stats", [P, TILES, 6], fp32)
        mean = sb("mean", [P, TILES], fp32)
        rstd = sb("rstd", [P, TILES], fp32)
        tmp = sb("tmp", [P, 4, TILES], fp32)
        ss = sb("ss", [P, TILES, 2], fp32)
        rn = sb("rn", [P, TILES, 2], fp32)
        payf = pay[:, :, :, :, :].rearrange("p a b c d -> p (a b c d)")
        sq = payf[:, 0:2 * D].rearrange("p (s n) -> p s n", s=2)
        ft = payf[:, 2 * D:4 * D].rearrange("p (s n) -> p s n", s=2)
        hl = payf[:, 4 * D:8 * D].bitcast(fp16).rearrange("p (s q n) -> p s q n", s=2, q=4)
        guard = sb("guard", [P, 2], fp32)
        den = sb("den", [P, 2, 2], fp32)
        g_sb = sb("g_sb", [P, 3, 2, D], fp32)
        v_sb = sb("v_sb", [P, 2, D], fp32)
        st2 = sb("st2", [P, 2, 6], fp32)
        mv2 = sb("mv2", [P, 2, 2], fp32)
        ve2 = sb("ve2", [P, 2], fp32)
        r2 = sb("r2", [P, 2], fp32)
        zt = sb("zt", [P, 2, P], fp32)
        lg = sb("lg", [P, 2, N_EXP], fp32)
        top = sb("top", [P, 2, 8], fp32)
        tix = sb("tix", [P, 2, 8], u32)
        tixf = sb("tixf", [P, 2, 2], fp32)
        oh = sb("oh", [P, 2, 2, N_EXP], fp32)
        ohg = sb("ohg", [P, 2, 2, N_EXP], fp32)
        comb = sb("comb", [P, 2, N_EXP], fp32)
        combt = sb("combt", [N_EXP, 2, P], fp32)
        csum = sb("csum", [P, N_EXP], bf16)
        gap = sb("gap", [P, 2], fp32)
        eg = sb("eg", [P, 2], fp32)
        eg1 = sb("eg1", [P, 2], fp32)
        place = sb("place", [P, 2, N_EXP], fp32)
        pos = sb("pos", [P, 2, 2], fp32)
        posi = sb("posi", [P, 2, 2, 2], i32)
        gf = g_sb[:, :, :, :].rearrange("p a t d -> p (a t d)")
        cnt, ntf, cin, cex, ind, ind2, junk = (gf[:, n * N_EXP:(n + 1) * N_EXP] for n in range(7))
        cnti, nti = (gf[:, n * N_EXP:(n + 1) * N_EXP].bitcast(i32) for n in (7, 8))
        tv = sb("tv", [P, 16], fp32)
        table = sb("table", [1, 3 * P], i32)
        p32f = p32[:, :, :].rearrange("p r n -> p (r n)")
        xt = p32f[:, 0:2 * P].rearrange("p (s n) -> p s n", s=2)
        w1s = p32f[:, 2 * P:2 * P + 2 * W1C].rearrange("p (s n) -> p s n", s=2)
        ht = p32f[:, 6 * P + 4:10 * P + 4].rearrange("p (s h n) -> p s h n", s=2, h=2)
        xg = phi[:, :, :].rearrange("p r n -> p (r n)").bitcast(fp32)[:, 0:4 * (D + 1)]\
            .rearrange("p (s n) -> p s n", s=4)
        ys = plo[:, :, :].rearrange("p r n -> p (r n)").bitcast(fp32)[:, 0:4 * D].rearrange("p (s n) -> p s n", s=4)

        def scratch(name, rows, cols):
            t = nc.dram_tensor(name, [rows, cols], fp32)
            return t.ap()

        xs = scratch("xs", XS_ROWS, D + 1)
        yt = scratch("yt", YT_ROWS, D)

        score = [ctx.enter_context(nc.psum_tensor(f"score{i}", [P, 512], fp32)) for i in range(3)]
        acc = [ctx.enter_context(nc.psum_tensor(f"acc{i}", [P, 2, 512], fp32)) for i in range(2)]
        route = ctx.enter_context(nc.psum_tensor("route", [P, 512], fp32))
        ftp = [score[0], score[1]]
        qkp = [acc[0][:, 0, :], acc[0][:, 1, :]]
        qtp = [acc[1][:, c, :].bitcast(fp16)[:, 0:512].rearrange("p (q n) -> p q n", q=4) for c in range(2)]
        xtp = [score[0], score[1]]
        hp = [[acc[0][:, 0, :], acc[0][:, 1, :]], [acc[1][:, 0, :], acc[1][:, 1, :]]]
        yp = [score[2], route]

        x_in_s = sem("x_loaded")
        w_in_s = sem("weights_loaded")
        adj_in_s = [sem(f"adj_loaded{s}") for s in range(2)]
        w1_in_s = sem("w1_loaded")
        w2_in_s = sem("w2_loaded")
        const_s = sem("constants_made")
        chain_s = sem("dve_step")
        pchain_s = sem("pool_step")
        pstep_s = sem("pool_route_step")
        bn_s = sem("x_row_stats")
        hi_s = sem("high_parts_made")
        half_s = sem("first_choice_added")
        st2_s = sem("x1_row_stats")
        lgb_s = sem("logits_biased")
        ypad_s = sem("y_padding_made")
        stats_s = sem("stats_made")
        rstd_s = sem("rstd_made")
        f_s = sem("f_made")
        fx_s = sem("fx_made")
        ftp_s = sem("f_transposed")
        ft_s = sem("f_transposed_copied")
        qk_s = sem("qk_projected")
        qk32_s = sem("qk_copied")
        ss_s = sem("squares_summed")
        rn_s = sem("row_norms_made")
        hl_s = sem("qk_split")
        qt_s = sem("qk_transposed")
        qtc_s = sem("qk_transposed_copied")
        mask_s = sem("mask_made")
        score_s = sem("scores_made")
        exp_s = sem("exponentials_made")
        lo_s = sem("low_parts_made")
        pv_s = sem("pair_accumulated")
        den_s = sem("guards_made")
        u_s = sem("residual_made")
        accread_s = sem("accumulators_read")
        mv_s = sem("moments_made")
        r2_s = sem("rstd2_made")
        z_s = sem("z_made")
        pay_s = sem("payload_made")
        ztp_s = sem("z_transposed")
        zt_s = sem("z_transposed_copied")
        lg_s = sem("logits_made")
        cho_s = sem("choices_made")
        eg_s = sem("gate_exponentials_made")
        cmb_s = sem("combine_made")
        rank_s = sem("ranks_made")
        pos_s = sem("positions_made")
        cbt_s = sem("combine_transposed")
        cbc_s = sem("combine_transposed_copied")
        b2_s = sem("b2_share_made")
        b2a_s = sem("b2_share_added")
        scat_s = [sem(f"rows_scattered{c}") for c in range(2)]
        cnt_s = sem("counts_made")
        tv_s = sem("table_columns_made")
        tr_s = sem("table_rows_made")
        tab_s = sem("table_made")
        padw_s = [sem(f"padding_written{c}") for c in range(4)]
        xg_s = [sem(f"tile_loaded{c}") for c in range(4)]
        xtp_s = sem("tile_transposed")
        xt_s = sem("tile_transposed_copied")
        w1s_s = sem("w1_picked")
        hp_s = sem("hidden_made")
        h0_s = sem("hidden0_activated")
        h1_s = sem("hidden1_activated")
        yp_s = sem("results_made")
        ys_s = [sem(f"results_copied{c}") for c in range(4)]
        ysc_s = [sem(f"results_scattered{c}") for c in range(4)]
        y_in_s = [sem(f"y_loaded{c}") for c in range(2)]
        out_s = sem("combined")
        st_s = sem("stored")

        def slot(b_odd, k):
            return (k + b_odd) % 3

        def since(b_odd, k):
            n = 1
            while True:
                q = k - n
                odd = b_odd if q >= 0 else 1 - b_odd
                if slot(odd, q % PAIRS) == slot(b_odd, k):
                    return n
                n += 1

        def at_once(eng):
            eng.wait_ge(const_s, 1)

        block = ctx.enter_context(nc.Block())

        @block.sync
        def _(sp):
            for c in range(2):
                half = slice(c * (TILES // 2), (c + 1) * (TILES // 2))
                sp.dma_start(x_sb[:, half, :], x_in[:, half, :]).then_inc(x_in_s, 16)

            def load_adj(t, s):
                sp.dma_start(raw[:, s, :], adj_in[ds(t * P, P), :]).then_inc(adj_in_s[s], 16)

            for s in range(2):
                load_adj(s, s)
            W1P = N_EXP * W1C // 8
            with sp.Fori(1, 9) as b:
                for s in range(2):
                    sp.wait_ge(mask_s, b * 2 + (s - 1))
                    load_adj(b * 2 + s, s)
                sp.wait_ge(qtc_s, TILES + 2)
                sp.wait_ge(fx_s, 1)
                sp.dma_start(w1_sb[:, ds((b - 1) * W1P, W1P)], w1_in[:, ds((b - 1) * W1P, W1P)])\
                  .then_inc(w1_in_s, 16)
            with sp.Fori(9, BLOCKS) as b:
                for s in range(2):
                    sp.wait_ge(mask_s, b * 2 + (s - 1))
                    load_adj(b * 2 + s, s)
            sp.wait_ge(mask_s, TILES)
            cut = 2 * NPAD
            sp.dma_start(w2_sb[:, 0:cut], w2_in[:, 0:cut]).then_inc(w2_in_s, 16)
            sp.wait_ge(pv_s, BLOCKS * PAIRS + 3)
            sp.dma_start(w2_sb[:, cut:N_EXP * HID], w2_in[:, cut:N_EXP * HID]).then_inc(w2_in_s, 16)
            sp.wait_ge(tab_s, 1)
            for c in range(2):
                sp.wait_ge(scat_s[c], 64 * (BLOCKS // 2 + (1 - c)))

            def write_padding(s, c):
                row = sp.value_load(table[0:1, ds(s + 2 * P, 1)], min_val=0, max_val=XS_ROWS - P)
                sp.dma_start(xs[ds(row, P), :], padrow[:, :]).then_inc(padw_s[c], 16)

            def load_tile(s, c, nth):
                sp.wait_ge(padw_s[c], nth * 16)
                row = sp.value_load(table[0:1, ds(s + P, 1)], min_val=0, max_val=XS_ROWS - P)
                sp.dma_start(xg[:, c, :], xs[ds(row, P), :]).then_inc(xg_s[c], 16)

            for c in range(4):
                write_padding(c, c)
            for c in range(4):
                load_tile(c, c, 1)
                write_padding(c + 4, c)
            with sp.Fori(1, FTILES // 4 - 1) as it:
                for c in range(4):
                    sp.wait_ge(ysc_s[c], it * 16)
                    load_tile(it * 4 + c, c, it + 1)
                    write_padding(it * 4 + (c + 4), c)
            for c in range(4):
                n = FTILES // 4 - 1
                sp.wait_ge(ysc_s[c], n * 16)
                load_tile(n * 4 + c, c, n + 1)
            for c in range(4):
                sp.wait_ge(ysc_s[c], FTILES // 4 * 16)
            sp.wait_ge(ypad_s, 1)
            for h in range(2):
                t0, t1 = h * 13, (h + 1) * 13
                for c in range(2):
                    src = yt[c * NPAD:(c + 1) * NPAD, :].rearrange("(t p) d -> p t d", p=P)
                    if h == 0:
                        sp.dma_start(y_sb[c][:, t0:t1, :], src[:, t0:t1, :]).then_inc(y_in_s[h], 16)
                    else:
                        sp.dma_start(y_sb[c][:, t0:t1 - 1, :], src[:, t0:t1 - 1, :]).then_inc(y_in_s[h], 16)
                        sp.dma_start(y_sb[c][0:112, t1 - 1, :], src[0:112, t1 - 1, :]).then_inc(y_in_s[h], 16)
                        sp.dma_start(y_sb[c][112:127, t1 - 1, :], src[112:127, t1 - 1, :]).then_inc(y_in_s[h], 16)
            for h in range(2):
                sp.wait_ge(out_s, 13 * (h + 1))
                sp.dma_start(out[:, h * 13:(h + 1) * 13, :], x_sb[:, h * 13:(h + 1) * 13, :]).then_inc(st_s, 16)
            sp.wait_ge(st_s, 32)

        @block.gpsimd
        def _(pool):
            count = [0]

            def link(ins):
                count[0] += 1
                ins.then_inc(pchain_s, 1)
                pool.wait_ge(pchain_s, count[0])

            link(pool.memset(m_half[:, :], -0.5))
            for m in (id32, id16, idm):
                link(pool.memset(m[:, :], 0.0))
                link(pool.affine_select(out=m[:, :], in_=m[:, :], compare_op=ALU.not_equal,
                                        fill=32768.0 if m is idm else 1.0,
                                        base=0, pattern=[[-1, P]], channel_multiplier=1))
            link(pool.memset(ones[:, :], 1.0))
            link(pool.affine_select(out=tri[:, :], in_=ones[:, :], compare_op=ALU.is_gt, fill=0.0,
                                    base=0, pattern=[[1, P]], channel_multiplier=-1))
            link(pool.memset(csum[:, :], 0.0))
            link(pool.memset(zero_e[:, :], 0.0))
            link(pool.memset(padrow[:, :], 0.0))
            link(pool.iota(iota_e[:, :], [[1, N_EXP]], base=0, channel_multiplier=0,
                           allow_small_or_imprecise_dtypes=True))
            link(pool.iota(dest[:, :, :], [[NPAD, 2], [P, TILES]], base=0, channel_multiplier=1))
            link(pool.iota(tok[:, :], [[P, TILES]], base=0, channel_multiplier=1,
                           allow_small_or_imprecise_dtypes=True))
            link(pool.iota(srow[:, :], [[0, 1]], base=0, channel_multiplier=1,
                           allow_small_or_imprecise_dtypes=True))
            link(pool.iota(padrow[:, D:D + 1].bitcast(i32), [[0, 1]], base=NOWHERE, channel_multiplier=0))
            link(pool.tensor_scalar(region[:, :], iota_e[:, :], float(CAP), None, ALU.mult))
            link(pool.tensor_scalar(padx[:, :], tok[:, :], float(N_TOK), float(NOWHERE), ALU.is_ge, ALU.mult))
            pool.tensor_scalar(spare[:, :], srow[:, :], float(P), float(SPARE), ALU.mult, ALU.add)\
                .then_inc(const_s, 1)

            pool.wait_ge(stats_s, 1)
            link(pool.tensor_scalar(tmp[:, 3, :], tmp[:, 2, :], EPS, None, ALU.add))
            pool.tensor_tensor(rstd[:, :], tmp[:, 3, :], m_half[:, 0:TILES], ALU.pow).then_inc(rstd_s, 1)

            pool.wait_ge(ss_s, 2 * TILES + 1)
            rn_flat = rn[:, :, :].rearrange("p t q -> p (t q)")
            ss_flat = ss[:, :, :].rearrange("p t q -> p (t q)")
            link(pool.tensor_scalar(ss_flat, ss_flat, 1e-8, None, ALU.max))
            pool.tensor_tensor(rn_flat, ss_flat, m_half[:, :], ALU.pow).then_inc(rn_s, 1)

            def residual(e, odd):
                fx2 = fx[:, ds(e * 2, 2), :]
                pool.wait_ge(fx_s, 1)
                pool.tensor_tensor(g_sb[:, 0], fx2[:, :, 0:D], fx2[:, :, D:2 * D], ALU.add).then_inc(pstep_s, 1)
                pool.wait_ge(den_s, e + 1)
                pool.wait_ge(pstep_s, e * 4 + 1)
                pool.tensor_tensor(g_sb[:, 1], g_sb[:, 0], guard[:, :, None].to_broadcast([P, 2, D]), ALU.mult)\
                    .then_inc(pstep_s, 1)
                pool.wait_ge(pstep_s, e * 4 + 2)
                pool.tensor_tensor(g_sb[:, 2], g_sb[:, 1], x_sb[:, ds(e * 2, 2), :], ALU.add).then_inc(u_s, 1)

            def second_norm(e, odd):
                at_once(pool)
                pool.wait_ge(mv_s, e + 1)
                pool.tensor_scalar(ve2[:, :], mv2[:, :, 1], EPS, None, ALU.add).then_inc(pstep_s, 1)
                pool.wait_ge(pstep_s, e * 4 + 3)
                pool.tensor_tensor(r2[:, :], ve2[:, :], m_half[:, 0:2], ALU.pow).then_inc(r2_s, 1)

            def payload(e, odd):
                pool.tensor_copy(pay[:, odd, :, :, D:D + 1].bitcast(i32),
                                 dest[:, :, ds(e * 2, 2)].rearrange("p c t -> p t c")[:, :, :, None])\
                    .then_inc(pstep_s, 1)
                at_once(pool)
                pool.wait_ge(z_s, e + 1)
                pool.tensor_copy(pay[:, odd, :, 1, 0:D], pay[:, odd, :, 0, 0:D]).then_inc(pay_s, 1)

            def scatters(e, odd):
                at_once(pool)
                pool.wait_ge(pos_s, e + 1)
                pool.wait_ge(pay_s, e + 1)
                for t in range(2):
                    for c in range(2):
                        pool.indirect_dma_start(
                            out=xs[:, :], out_offset=bass.IndirectOffsetOnAxis(ap=posi[:, odd, t, c:c + 1], axis=0),
                            in_=pay[:, odd, t, c, :], in_offset=None,
                            bounds_check=XS_ROWS - 1, oob_is_err=False).then_inc(scat_s[odd], 16)

            pool.wait_ge(const_s, 1)

            def body(e, odd, again=True):
                residual(e, odd)
                second_norm(e, odd)
                at_once(pool)
                if again:
                    pool.wait_ge(scat_s[odd], (e - odd) * 32)
                payload(e, odd)
                scatters(e, odd)

            body(0, 0, again=False)
            body(1, 1, again=False)
            with pool.Fori(1, (BLOCKS - 1) // 2) as it:
                for u in range(2):
                    body(it * 2 + u, u)
            body(BLOCKS - 1, 0)

            def send(nth, c):
                at_once(pool)
                pool.wait_ge(ys_s[c], nth)
                pool.indirect_dma_start(
                    out=yt[:, :], out_offset=bass.IndirectOffsetOnAxis(ap=xg[:, c, D:D + 1].bitcast(i32), axis=0),
                    in_=ys[:, c, :], in_offset=None, bounds_check=YT_ROWS - 1, oob_is_err=False)\
                    .then_inc(ysc_s[c], 16)

            with pool.Fori(1, FTILES // 4 + 1) as nth:
                for c in range(4):
                    send(nth, c)

        @block.tensor
        def _(pe):
            mm = nc.tensor.matmul
            pe.sem_inc(qk_s, 2)
            pe.sem_inc(qt_s, 2)
            pe.wait_ge(const_s, 1)
            pe.wait_ge(w_in_s, 64)

            def project(t, u):
                pe.wait_ge(ft_s, t + 3)
                pe.wait_ge(qk32_s, t + 1)
                mm(qkp[u][:, 0:2 * D], ft[:, u, :], wqk[:, :], start=True, stop=True).then_inc(qk_s, 1)

            for it in range(TILES // 2):
                for u in range(2):
                    pe.wait_ge(f_s, it * 2 + u + 1)
                    pe.wait_ge(ft_s, it * 2 + u + 1)
                    nc.tensor.transpose(ftp[u][:, 0:P], f32_sb[:, it * 2 + u, :], id32[:, :]).then_inc(ftp_s, 1)
                for u in range(2):
                    project(it * 2 + u, u)
            with pe.Fori(0, TILES // 2) as it:
                for u in range(2):
                    pe.wait_ge(hl_s, it * 2 + (u + 1))
                    pe.wait_ge(qtc_s, it * 2 + (u + 1))
                    for q in range(4):
                        last = nc.tensor.transpose(qtp[u][:, q, :], hl[:, u, q, :], id16[:, :])
                    last.then_inc(qt_s, 1)

            def scores(b, odd, k):
                p = b * PAIRS + k
                r = slot(odd, k)
                if k == 0:
                    pe.wait_ge(mask_s, b * 2 + 2)
                pe.wait_ge(exp_s, p - since(odd, k) + 4)
                for j in range(2):
                    o = score[r][:, 256 * j:256 * j + 256]
                    cols = slice((2 * k + j) * P, (2 * k + j + 1) * P)
                    for i in range(2):
                        mm(o[:, P * i:P * i + P], mask[:, 2 * odd + i, cols], idm[:, :],
                           start=(j == 0 and i == 0), stop=False, skip_group_check=True)
                    for n, (a, c) in enumerate(((0, 2), (0, 3), (1, 2))):
                        last = mm(o, qk[:, a, cols], qk[:, c, ds(b * 256, 256)],
                                  start=False, stop=(n == 2 and j == 1), skip_group_check=True)
                last.then_inc(score_s, 1)

            def accumulate(b, odd, k):
                p = b * PAIRS + k
                r = slot(odd, k)
                if k == 0 and not (isinstance(b, int) and b < 2):
                    pe.wait_ge(accread_s, b - 1)
                pe.wait_ge(lo_s, p + 1)
                for j in range(2):
                    t = 2 * k + j
                    for i in range(2):
                        w = slice(256 * j + P * i, 256 * j + P * i + P)
                        mm(acc[odd][:, i, 0:FXC], phi[:, r, w], fx[:, t, :],
                           start=(t == 0), stop=False, skip_group_check=True)
                        last = mm(acc[odd][:, i, D:FXC], plo[:, r, w], fx[:, t, D:FXC],
                                  start=False, stop=(t == TILES - 1), skip_group_check=True)
                last.then_inc(pv_s, 1)

            def route_zt(e, odd):
                pe.wait_ge(z_s, e + 1)
                pe.wait_ge(b2a_s, e)
                for t in range(2):
                    last = nc.tensor.transpose(route[:, P * t:P * t + P], pay[:, odd, t, 0, 0:D], id32[:, :])
                last.then_inc(ztp_s, 1)

            def route_logits(e):
                pe.wait_ge(zt_s, e + 1)
                for t in range(2):
                    last = mm(route[:, 256 + 64 * t:320 + 64 * t], zt[:, t, :], wr[:, :], start=True, stop=True)
                last.then_inc(lg_s, 1)

            def route_ranks(e, odd):
                pe.wait_ge(cho_s, e + 1)
                for t in range(2):
                    o = route[:, 384 + 64 * t:448 + 64 * t]
                    mm(o, tri[:, :], c_all[:, odd, t, :], start=True, stop=False)
                    last = mm(o, ones[:, :], csum[:, :], start=False, stop=(t == 0))
                    if t == 1:
                        last = mm(o, ones[:, :], c_all[:, odd, 0, :], start=False, stop=True)
                last.then_inc(rank_s, 1)

            def route_combine(e):
                at_once(pe)
                pe.wait_ge(cmb_s, e + 1)
                pe.wait_ge(pos_s, e + 1)
                for t in range(2):
                    last = nc.tensor.transpose(route[0:N_EXP, P * t:P * t + P], comb[:, t, :], id32[:, :])
                last.then_inc(cbt_s, 1)

            def route_b2(e):
                pe.wait_ge(cbc_s, e + 1)
                for t in range(2):
                    last = mm(route[:, 256 + P * t:384 + P * t], combt[:, t, :], b2[:, :], start=True, stop=True)
                last.then_inc(b2_s, 1)

            def route_step(e, odd, k):
                if k == 4:
                    route_zt(e, odd)
                if k == 6:
                    route_logits(e)
                if k == 8:
                    route_ranks(e, odd)
                if k == 11:
                    route_combine(e)

            pe.wait_ge(qtc_s, TILES + 2)
            pe.wait_ge(fx_s, 1)
            scores(0, 0, 0)
            scores(0, 0, 1)

            def body(b, odd, routed=True, late=True, ahead=True):
                for k in range(PAIRS):
                    if k + 2 < PAIRS:
                        scores(b, odd, k + 2)
                    elif ahead:
                        scores(b + 1, 1 - odd, k + 2 - PAIRS)
                    accumulate(b, odd, k)
                    if late and k == 1:
                        route_b2(b - 2)
                    if routed:
                        route_step(b - 1, 1 - odd, k)

            body(0, 0, routed=False, late=False)
            body(1, 1, late=False)
            with pe.Fori(1, (BLOCKS - 1) // 2) as it:
                for u in range(2):
                    body(it * 2 + u, u)
            body(BLOCKS - 1, 0, ahead=False)
            route_b2(BLOCKS - 2)
            for k in range(PAIRS):
                route_step(BLOCKS - 1, 0, k)
            route_b2(BLOCKS - 1)
            pe.wait_ge(b2a_s, BLOCKS)
            mm(route[:, 0:N_EXP], ones[:, :], csum[:, :], start=True, stop=True).then_inc(cnt_s, 1)
            pe.wait_ge(tv_s, 1)
            for c in range(3):
                last = mm(route[0:1, P * c:P * c + P], tv[:, c:c + 1], id32[:, :], start=True, stop=True)
            last.then_inc(tr_s, 1)
            pe.wait_ge(tab_s, 1)
            pe.wait_ge(w2_in_s, 32)

            def transpose_tile(s, c, nth):
                pe.wait_ge(xg_s[c], nth * 16)
                pe.wait_ge(xt_s, s + 1)
                nc.tensor.transpose(xtp[c % 2][:, 0:P], xg[:, c, 0:D], id32[:, :]).then_inc(xtp_s, 1)

            def hidden(s, c):
                pe.wait_ge(xt_s, s + 3)
                pe.wait_ge(w1s_s, s + 1)
                pe.wait_ge(h0_s, s + 1)
                pe.wait_ge(h1_s, s + 1)
                for h in range(2):
                    last = mm(hp[c % 2][h][:, 0:P], w1s[:, c % 2, P * h:P * h + P], xt[:, c % 2, :],
                              start=True, stop=True)
                last.then_inc(hp_s, 1)

            transpose_tile(0, 0, 1)
            transpose_tile(1, 1, 1)
            hidden(0, 0)

            def tile_step(s, c, nth, waits=True, more=2):
                if more > 1:
                    transpose_tile(s + 2, (c + 2) % 4, nth + (1 if c >= 2 else 0))
                if more > 0:
                    hidden(s + 1, (c + 1) % 4)
                e = pe.value_load(table[0:1, ds(s, 1)], min_val=0, max_val=N_EXP - 1)
                pe.wait_ge(h0_s, s + 3)
                pe.wait_ge(h1_s, s + 3)
                if waits:
                    pe.wait_ge(ys_s[(c + 2) % 4], nth if c >= 2 else nth - 1)
                for h in range(2):
                    last = mm(yp[c % 2][:, 0:D], ht[:, c % 2, h, :], w2_sb[:, ds(e * HID + P * h, P)],
                              start=(h == 0), stop=(h == 1))
                last.then_inc(yp_s, 1)

            for c in range(4):
                tile_step(c, c, 1, waits=c >= 2)
            with pe.Fori(1, FTILES // 4 - 1) as it:
                for c in range(4):
                    tile_step(it * 4 + c, c, it + 1)
            for c in range(4):
                tile_step(FTILES - 4 + c, c, FTILES // 4, more=min(2, 3 - c))

        @block.scalar
        def _(act):
            A = nc.scalar.activation
            act.dma_start(wqk[:, :], wqk_in[:, :]).then_inc(w_in_s, 16)
            act.dma_start(wr[:, :], wr_in[:, :]).then_inc(w_in_s, 16)
            act.dma_start(br[:, :], br_in[:, :]).then_inc(w_in_s, 16)
            act.dma_start(b2[:, :], b2_in[:, :]).then_inc(w_in_s, 16)
            act.sem_inc(ft_s, 2)
            act.sem_inc(qtc_s, 2)
            act.sem_inc(exp_s, 3)
            act.sem_inc(ss_s, 1)
            act.sem_inc(xt_s, 2)
            act.sem_inc(h0_s, 2)

            with act.Fori(0, TILES // 2) as it:
                for u in range(2):
                    act.wait_ge(ftp_s, it * 2 + (u + 1))
                    act.wait_ge(qk_s, it * 2 + (u + 1))
                    A(ft[:, u, :], ftp[u][:, 0:P], ACT.Copy).then_inc(ft_s, 1)
                for u in range(2):
                    act.wait_ge(qk32_s, it * 2 + (u + 3))
                    for q in range(2):
                        act.wait_ge(ss_s, it * 4 + (2 * u + q + 1))
                        A(sq[:, 1, :], qk32[:, ds(it * 2 + u, 1), q, :], ACT.Square,
                          accum_out=ss[:, ds(it * 2 + u, 1), q]).then_inc(ss_s, 1)
            with act.Fori(0, TILES // 2) as it:
                for u in range(2):
                    act.wait_ge(qt_s, it * 2 + (u + 3))
                    A(qk[:, :, ds(it * 256 + P * u, P)], qtp[u], ACT.Copy).then_inc(qtc_s, 1)

            def exps(b, odd, k):
                p = b * PAIRS + k
                r = slot(odd, k)
                act.wait_ge(score_s, p + 1)
                act.wait_ge(pv_s, p - since(odd, k) + 4)
                A(p32[:, r, :], score[r][:, :], ACT.Exp)
                A(phi[:, r, :], score[r][:, :], ACT.Exp).then_inc(exp_s, 1)

            def route_step(e, k):
                if k == 6:
                    act.wait_ge(ztp_s, e + 1)
                    A(zt[:, :, :], route[:, 0:256].rearrange("p (t n) -> p t n", t=2), ACT.Copy).then_inc(zt_s, 1)
                if k == 10:
                    act.wait_ge(cho_s, e + 1)
                    A(eg[:, :], gap[:, :], ACT.Exp).then_inc(eg_s, 1)

            def body(b, odd, routed=True):
                for k in range(PAIRS):
                    exps(b, odd, k)
                    if routed:
                        route_step(b - 1, k)

            body(0, 0, routed=False)
            body(1, 1)
            with act.Fori(1, (BLOCKS - 1) // 2) as it:
                for u in range(2):
                    body(it * 2 + u, u)
            body(BLOCKS - 1, 0)
            for k in range(PAIRS):
                route_step(BLOCKS - 1, k)

            def tile_in(s, c):
                act.wait_ge(xtp_s, s + 1)
                act.wait_ge(hp_s, s - 1)
                A(xt[:, c % 2, :], xtp[c % 2][:, 0:P], ACT.Copy).then_inc(xt_s, 1)

            def relu(s, c, early):
                act.wait_ge(hp_s, s + 1)
                if not early:
                    act.wait_ge(yp_s, s - 1)
                A(ht[:, c % 2, 0, :], hp[c % 2][0][:, 0:P], ACT.Relu, bias=w1s[:, c % 2, HID:HID + 1])\
                    .then_inc(h0_s, 1)

            def result(s, c, it16):
                act.wait_ge(yp_s, s + 1)
                if it16 is not None:
                    act.wait_ge(ysc_s[c], it16)
                A(ys[:, c, :], yp[c % 2][:, 0:D], ACT.Copy).then_inc(ys_s[c], 1)

            act.wait_ge(xtp_s, 1)
            A(xt[:, 0, :], xtp[0][:, 0:P], ACT.Copy).then_inc(xt_s, 1)
            act.wait_ge(xtp_s, 2)
            A(xt[:, 1, :], xtp[1][:, 0:P], ACT.Copy).then_inc(xt_s, 1)
            relu(0, 0, True)

            def tile_step(s, c, early=False, it16=None, more=2):
                if more > 1:
                    tile_in(s + 2, (c + 2) % 4)
                if more > 0:
                    relu(s + 1, (c + 1) % 4, early)
                result(s, c, it16)

            for c in range(4):
                tile_step(c, c, early=c == 0)
            with act.Fori(1, FTILES // 4 - 1) as it:
                for c in range(4):
                    tile_step(it * 4 + c, c, it16=it * 16)
            for c in range(4):
                tile_step(FTILES - 4 + c, c, it16=(FTILES // 4 - 1) * 16, more=min(2, 3 - c))

        @block.vector
        def _(dve):
            V = nc.vector
            count = [0, 0]

            def link(ins):
                count[0] += 1
                ins.then_inc(chain_s, 1)
                dve.wait_ge(chain_s, count[1] + count[0])

            dve.sem_inc(qk32_s, 2)
            dve.sem_inc(pv_s, 3)
            dve.sem_inc(h1_s, 2)
            V.memset(fx[:, :, 2 * D:FXC], 1.0)

            dve.wait_ge(x_in_s, 32)
            for c in range(2):
                with dve.Fori(13 * c, 13 * (c + 1)) as t:
                    V.bn_stats(stats[:, ds(t, 1), :], x_sb[:, ds(t, 1), :]).then_inc(bn_s, 1)
            dve.wait_ge(bn_s, TILES)
            even, odd_m = stats[:, :, 1], stats[:, :, 4]
            link(V.tensor_tensor(tmp[:, 0, :], even, odd_m, ALU.add))
            link(V.tensor_scalar(mean[:, :], tmp[:, 0, :], 0.5, None, ALU.mult))
            link(V.tensor_tensor(tmp[:, 1, :], even, odd_m, ALU.subtract))
            link(V.scalar_tensor_tensor(tmp[:, 0, :], tmp[:, 1, :], 0.25, tmp[:, 1, :], ALU.mult, ALU.mult))
            link(V.tensor_tensor(tmp[:, 1, :], stats[:, :, 2], stats[:, :, 5], ALU.add))
            V.scalar_tensor_tensor(tmp[:, 2, :], tmp[:, 1, :], 1.0 / D, tmp[:, 0, :], ALU.mult, ALU.add)\
             .then_inc(stats_s, 1)
            dve.wait_ge(rstd_s, 1)
            with dve.Fori(0, TILES) as t:
                V.tensor_scalar(f32_sb[:, ds(t, 1), :], x_sb[:, ds(t, 1), :], mean[:, ds(t, 1)], rstd[:, ds(t, 1)],
                                ALU.subtract, ALU.mult).then_inc(f_s, 1)
            with dve.Fori(0, TILES // 2) as it:
                for u in range(2):
                    dve.wait_ge(qk_s, it * 2 + (u + 3))
                    V.tensor_copy(qk32[:, ds(it * 2 + u, 1), :, :],
                                  qkp[u][:, 0:2 * D].rearrange("p (q h) -> p q h", q=2)).then_inc(qk32_s, 1)
            link(V.tensor_copy(fx[:, :, D:2 * D], f32_sb[:, :, :]))
            V.tensor_tensor(fx[:, :, 0:D], f32_sb[:, :, :], fx[:, :, D:2 * D], ALU.subtract).then_inc(fx_s, 1)

            def convert(t, slot_, s, part, parts):
                w = NPAD // parts
                cols = slice(part * w, (part + 1) * w)
                if part == 0:
                    dve.wait_ge(adj_in_s[s], (t - s) * 8 + 16)
                return V.tensor_scalar(mask[:, slot_, cols], raw[:, s, cols], 0.0, 1.0, ALU.is_gt, ALU.subtract)

            for s in range(2):
                convert(s, s, s, 0, 1).then_inc(mask_s, 1)
            dve.wait_ge(rn_s, 1)
            with dve.Fori(0, TILES // 2) as it:
                for u in range(2):
                    dve.wait_ge(qt_s, it * 2 + (u + 1))
                    for q in range(2):
                        V.tensor_scalar(hl[:, u, 2 * q, :], qk32[:, ds(it * 2 + u, 1), q, :],
                                        rn[:, ds(it * 2 + u, 1), q], None, ALU.mult).then_inc(hi_s, 1)
                    for q in range(2):
                        dve.wait_ge(hi_s, it * 4 + (2 * u + q + 1))
                        last = V.scalar_tensor_tensor(hl[:, u, 2 * q + 1, :], qk32[:, ds(it * 2 + u, 1), q, :],
                                                      rn[:, ds(it * 2 + u, 1), q], hl[:, u, 2 * q, :],
                                                      ALU.mult, ALU.subtract)
                    last.then_inc(hl_s, 1)

            dve.wait_ge(const_s, 1)
            dve.wait_ge(w_in_s, 64)

            def low(b, odd, k):
                p = b * PAIRS + k
                r = slot(odd, k)
                dve.wait_ge(exp_s, p + 4)
                V.tensor_tensor(plo[:, r, :], p32[:, r, :], phi[:, r, :], ALU.subtract).then_inc(lo_s, 1)

            def route_step(e, odd, k):
                a = acc[odd]
                tiles = ds(e * 2, 2)
                if k == 0:
                    dve.wait_ge(pv_s, e * PAIRS + (PAIRS + 3))
                    link(V.tensor_scalar(den[:, 0, :], a[:, :, 2 * D], 0.0, 0.5, ALU.is_le, ALU.mult))
                    V.tensor_scalar(guard[:, :], den[:, 0, :], 0.5, None, ALU.add).then_inc(den_s, 1)
                    link(V.tensor_scalar(den[:, 1, :], a[:, :, 2 * D], 1e-30, 2.0, ALU.max, ALU.mult))
                    link(V.reciprocal(den[:, 0, :], den[:, 1, :]))
                if k == 2:
                    dve.wait_ge(u_s, e + 1)
                    for t in range(2):
                        last = V.scalar_tensor_tensor(v_sb[:, t, :], a[:, t, 0:D], den[:, 0, t:t + 1],
                                                      g_sb[:, 2, t, :], ALU.mult, ALU.add)
                    link(last)
                    for t in range(2):
                        last = V.scalar_tensor_tensor(x_sb[:, ds(e * 2 + t, 1), :].rearrange("p o d -> p (o d)"),
                                                      a[:, t, D:2 * D], den[:, 0, t:t + 1],
                                                      v_sb[:, t, :], ALU.mult, ALU.add)
                    last.then_inc(accread_s, 1)
                    at_once(dve)
                    dve.wait_ge(accread_s, e + 1)
                    for t in range(2):
                        last = V.bn_stats(st2[:, t, :], x_sb[:, ds(e * 2 + t, 1), :])
                    last.then_inc(st2_s, 1)
                    at_once(dve)
                    dve.wait_ge(st2_s, e + 1)
                    for t in range(2):
                        last = V.bn_aggr(mv2[:, t, :], st2[:, t, :])
                    last.then_inc(mv_s, 1)
                if k == 4:
                    dve.wait_ge(r2_s, e + 1)
                    dve.wait_ge(pstep_s, e * 4 + 4)
                    for t in range(2):
                        last = V.tensor_scalar(pay[:, odd, t, 0, 0:D],
                                               x_sb[:, ds(e * 2 + t, 1), :],
                                               mv2[:, t, 0:1], r2[:, t:t + 1], ALU.subtract, ALU.mult)
                    last.then_inc(z_s, 1)
                if k == 8:
                    dve.wait_ge(lg_s, e + 1)
                    V.tensor_tensor(lg[:, :, :], route[:, 256:384].rearrange("p (t n) -> p t n", t=2),
                                    br[:, None, :].to_broadcast([P, 2, N_EXP]), ALU.add).then_inc(lgb_s, 1)
                    at_once(dve)
                    dve.wait_ge(lgb_s, e + 1)
                    for t in range(2):
                        last = V.max(top[:, t, :], lg[:, t, :])
                    link(last)
                    V.tensor_tensor(gap[:, :], top[:, :, 1], top[:, :, 0], ALU.subtract)
                    for t in range(2):
                        last = V.max_index(tix[:, t, :], top[:, t, :], lg[:, t, :])
                    link(last)
                    link(V.tensor_tensor(tixf[:, :, :], tix[:, :, 0:2],
                                         padx[:, tiles][:, :, None].to_broadcast([P, 2, 2]), ALU.add))
                    link(V.tensor_tensor(oh[:, :, :, :], iota_e[:, None, None, :].to_broadcast([P, 2, 2, N_EXP]),
                                         tixf[:, :, :, None].to_broadcast([P, 2, 2, N_EXP]), ALU.is_equal))
                    V.tensor_tensor(c_all[:, odd, :, :], oh[:, :, 0, :], oh[:, :, 1, :], ALU.add).then_inc(cho_s, 1)
                if k == 10:
                    dve.wait_ge(eg_s, e + 1)
                    link(V.tensor_scalar(eg1[:, :], eg[:, :], 1.0, None, ALU.add))
                    link(V.reciprocal(gates[:, tiles, 0], eg1[:, :]))
                    link(V.tensor_tensor(gates[:, tiles, 1], eg[:, :], gates[:, tiles, 0], ALU.mult))
                    link(V.tensor_tensor(ohg[:, :, :, :], oh[:, :, :, :],
                                         gates[:, tiles, :][:, :, :, None].to_broadcast([P, 2, 2, N_EXP]), ALU.mult))
                    V.tensor_tensor(comb[:, :, :], ohg[:, :, 0, :], ohg[:, :, 1, :], ALU.add).then_inc(cmb_s, 1)
                if k == 11:
                    dve.wait_ge(rank_s, e + 1)
                    link(V.tensor_tensor(place[:, :, :], route[:, 384:512].rearrange("p (t n) -> p t n", t=2),
                                         region[:, None, :].to_broadcast([P, 2, N_EXP]), ALU.add))
                    dve.wait_ge(cmb_s, e + 1)
                    link(V.tensor_tensor(ohg[:, :, :, :], oh[:, :, :, :],
                                         place[:, :, None, :].to_broadcast([P, 2, 2, N_EXP]), ALU.mult))
                    link(V.tensor_reduce(pos[:, :, :], ohg[:, :, :, :], AX.X, ALU.add))
                    V.tensor_tensor(posi[:, odd, :, :], pos[:, :, :],
                                    padx[:, tiles][:, :, None].to_broadcast([P, 2, 2]), ALU.add).then_inc(pos_s, 1)
                    link(V.tensor_tensor(csum[:, :], csum[:, :], c_all[:, odd, 0, :], ALU.add))
                    link(V.tensor_tensor(csum[:, :], csum[:, :], c_all[:, odd, 1, :], ALU.add))

            def combine_copy(e):
                dve.wait_ge(cbt_s, e + 1)
                V.tensor_copy(combt[:, :, :], route[0:N_EXP, 0:256].rearrange("p (t n) -> p t n", t=2))\
                 .then_inc(cbc_s, 1)

            def b2_add(e):
                dve.wait_ge(b2_s, e + 1)
                V.tensor_tensor(x_sb[:, ds(e * 2, 2), :], x_sb[:, ds(e * 2, 2), :],
                                route[:, 256:512].rearrange("p (t n) -> p t n", t=2), ALU.add).then_inc(b2a_s, 1)

            def body(b, odd, routed=True, late=True, conv=True):
                for k in range(PAIRS):
                    low(b, odd, k)
                    if late and k == 0:
                        combine_copy(b - 2)
                    if late and k == 3:
                        b2_add(b - 2)
                    if routed:
                        route_step(b - 1, 1 - odd, k)
                    if conv and k in (3, 5, 6, 7):
                        n = (3, 5, 6, 7).index(k)
                        c = convert(b * 2 + (2 + n // 2), 2 * (1 - odd) + n // 2, n // 2, n % 2, 2)
                        if n % 2:
                            c.then_inc(mask_s, 1)

            body(0, 0, routed=False, late=False)
            body(1, 1, late=False)
            start = count[0]
            with dve.Fori(1, (BLOCKS - 1) // 2) as it:
                count[1] = (it - 1) * LOOP_LINKS
                for u in range(2):
                    body(it * 2 + u, u)
            assert count[0] - start == LOOP_LINKS, count[0] - start
            count[1] = 0
            count[0] = start + ((BLOCKS - 1) // 2 - 1) * LOOP_LINKS
            body(BLOCKS - 1, 0, conv=False)
            combine_copy(BLOCKS - 2)
            b2_add(BLOCKS - 2)
            for k in range(PAIRS):
                route_step(BLOCKS - 1, 0, k)
            combine_copy(BLOCKS - 1)
            b2_add(BLOCKS - 1)

            dve.wait_ge(cnt_s, 1)
            link(V.tensor_copy(cnt[:, :], route[:, 0:N_EXP]))
            link(V.tensor_scalar(cnti[:, :], cnt[:, :], float(P - 1), None, ALU.add))
            link(V.tensor_scalar(nti[:, :], cnti[:, :], 7, None, ALU.arith_shift_right))
            link(V.tensor_copy(ntf[:, :], nti[:, :]))
            link(V.tensor_tensor_scan(cin[:, :], ntf[:, :], zero_e[:, :], 0.0, ALU.add, ALU.add))
            link(V.tensor_tensor(cex[:, :], cin[:, :], ntf[:, :], ALU.subtract))
            link(V.tensor_scalar(ind2[:, :], cin[:, :], srow[:, :], None, ALU.is_gt))
            link(V.scalar_tensor_tensor(ind[:, :], cex[:, :], srow[:, :], ind2[:, :], ALU.is_le, ALU.mult))
            def pick(col, values):
                link(V.tensor_tensor_reduce(out=junk[:, :], in0=ind[:, :], in1=values, scale=1.0, scalar=0.0,
                                            op0=ALU.mult, op1=ALU.add, accum_out=tv[:, col:col + 1]))
            pick(0, iota_e[:, :])
            pick(4, region[:, :])
            pick(5, cnt[:, :])
            pick(6, cex[:, :])
            pick(7, ind[:, :])
            c_ = lambda n: tv[:, n:n + 1]
            link(V.tensor_tensor(c_(8), srow[:, :], c_(6), ALU.subtract))
            link(V.scalar_tensor_tensor(c_(9), c_(8), float(P), c_(4), ALU.mult, ALU.add))
            link(V.tensor_tensor(c_(10), c_(4), c_(5), ALU.add))
            link(V.tensor_tensor(c_(11), c_(9), spare[:, :], ALU.subtract))
            link(V.scalar_tensor_tensor(c_(1), c_(11), c_(7), spare[:, :], ALU.mult, ALU.add))
            link(V.scalar_tensor_tensor(c_(12), c_(9), float(P), c_(10), ALU.add, ALU.is_ge))
            link(V.tensor_tensor(c_(13), c_(12), c_(7), ALU.mult))
            link(V.tensor_tensor(c_(14), c_(10), spare[:, :], ALU.subtract))
            link(V.scalar_tensor_tensor(c_(2), c_(14), c_(13), spare[:, :], ALU.mult, ALU.add))
            V.tensor_copy(c_(3), c_(2)).then_inc(tv_s, 1)
            dve.wait_ge(tr_s, 1)
            V.tensor_copy(table[:, :], route[0:1, 0:3 * P]).then_inc(tab_s, 1)
            dve.wait_ge(tab_s, 1)
            dve.wait_ge(w1_in_s, 128)

            def pick_w1(s, c, early):
                e = dve.value_load(table[0:1, ds(s, 1)], min_val=0, max_val=N_EXP - 1)
                if not early:
                    dve.wait_ge(hp_s, s - 1)
                    dve.wait_ge(h0_s, s + 1)
                    dve.wait_ge(h1_s, s + 1)
                V.tensor_copy(w1s[:, c % 2, :], w1_sb[:, ds(e * W1C, W1C)]).then_inc(w1s_s, 1)

            def relu(s, c, early):
                dve.wait_ge(hp_s, s + 1)
                if not early:
                    dve.wait_ge(yp_s, s - 1)
                dve.wait_ge(w1s_s, s + 1)
                V.tensor_scalar(ht[:, c % 2, 1, :], hp[c % 2][1][:, 0:P], w1s[:, c % 2, HID + 1:HID + 2], 0.0,
                                ALU.add, ALU.max).then_inc(h1_s, 1)

            pick_w1(0, 0, True)
            pick_w1(1, 1, True)
            relu(0, 0, True)
            pick_w1(2, 2, False)

            def tile_step(s, c, early=False, more=3):
                if more > 0:
                    relu(s + 1, (c + 1) % 4, early)
                if more > 2:
                    pick_w1(s + 3, (c + 3) % 4, False)

            for c in range(4):
                tile_step(c, c, early=c == 0)
            with dve.Fori(1, FTILES // 4 - 1) as it:
                for c in range(4):
                    tile_step(it * 4 + c, c)
            for c in range(4):
                tile_step(FTILES - 4 + c, c, more=3 - c)

            dve.wait_ge(hp_s, FTILES)
            dve.wait_ge(w1s_s, FTILES)
            for c in range(2):
                last = V.memset(y_sb[c][96:P, TILES - 1, :], 0.0)
            last.then_inc(ypad_s, 1)
            for h in range(2):
                dve.wait_ge(y_in_s[h], 32 if h == 0 else 96)
                with dve.Fori(13 * h, 13 * (h + 1)) as t:
                    row = x_sb[:, ds(t, 1), :]
                    V.scalar_tensor_tensor(row, y_sb[0][:, ds(t, 1), :], gates[:, ds(t, 1), 0], row,
                                           ALU.mult, ALU.add).then_inc(half_s, 1)
                    dve.wait_ge(half_s, t + 1)
                    V.scalar_tensor_tensor(row, y_sb[1][:, ds(t, 1), :], gates[:, ds(t, 1), 1], row,
                                           ALU.mult, ALU.add).then_inc(out_s, 1)



def kernel(x, adj, L0_gnn_Wq, L0_gnn_Wk, L0_ffn_Wr, L0_ffn_br, L0_ffn_W1, L0_ffn_b1, L0_ffn_W2, L0_ffn_b2):
    import numpy as np
    import concourse.bacc as bacc
    from concourse import mybir as mb
    from concourse.bass_utils import run_bass_kernel_spmd

    x, adj, wq, wk, wr, br, w1, b1, w2, b2 = (np.asarray(a) for a in (
        x, adj, L0_gnn_Wq, L0_gnn_Wk, L0_ffn_Wr, L0_ffn_br, L0_ffn_W1, L0_ffn_b1, L0_ffn_W2, L0_ffn_b2))
    xp = np.zeros((NPAD, D), x.dtype)
    xp[:N_TOK] = x
    ap = np.zeros((NPAD, NPAD), adj.dtype)
    ap[:N_TOK, :N_TOK] = adj
    w1p = np.concatenate([w1.transpose(1, 0, 2), b1.reshape(N_EXP, 2, P).transpose(2, 0, 1)], axis=2)
    arrays = {
        "x_in": xp.reshape(TILES, P, D).transpose(1, 0, 2),
        "adj_in": ap,
        "wqk_in": np.concatenate([wq.T, wk.T], axis=1),
        "wr_in": wr,
        "br_in": np.broadcast_to(br[None, :], (P, N_EXP)),
        "w1_in": w1p.reshape(P, N_EXP * W1C),
        "w2_in": w2.reshape(N_EXP, 2, P, D).transpose(2, 0, 1, 3).reshape(P, N_EXP * HID),
        "b2_in": b2,
    }
    arrays = {n: np.ascontiguousarray(a) for n, a in arrays.items()}
    nc = bacc.Bacc("TRN2", target_bir_lowering=False, num_devices=1)
    args = [nc.dram_tensor(n, a.shape, mb.dt.from_np(a.dtype), kind="ExternalInput").ap() for n, a in arrays.items()]
    out = nc.dram_tensor("out", (P, TILES, D), mb.dt.float32, kind="ExternalOutput").ap()
    gnn_moe_program(nc, *args, out)
    r = run_bass_kernel_spmd(nc, [arrays], core_ids=[0])
    got = r.results[0]["out"]
    return got.transpose(1, 0, 2).reshape(NPAD, D)[:N_TOK]
```

```python
import concourse.bass as bass
from concourse import mybir
from contextlib import ExitStack

N_TOK, D, HID, N_EXP = 3327, 128, 256, 64
P = 128
TILES = -(-N_TOK // P)
NPAD = TILES * P
BLOCKS = TILES // 2
PAIRS = TILES // 2
CAP = NPAD + P
FTILES = 116
RING = 12
TURNS = FTILES // RING
REST = FTILES - TURNS * RING
XS_ROWS = N_EXP * CAP
YT_ROWS = 2 * NPAD
NOWHERE = 1 << 20
EPS = 1e-5
W1C = HID + 2
FXC = 2 * D + 1
LOOP_LINKS = 34
CHUNKS = ((0, 7), (7, 14), (14, 20), (20, TILES))
BIG = 3 * NPAD * 2


def gnn_moe_program(nc, x_in, adj_in, wqk_in, wr_in, br_in, w1_in, w2_in, b2_in, out):
    fp32, bf16, fp16 = mybir.dt.float32, mybir.dt.bfloat16, mybir.dt.float16
    i32, u32 = mybir.dt.int32, mybir.dt.uint32
    ALU, ACT, AX = mybir.AluOpType, mybir.ActivationFunctionType, mybir.AxisListType
    ds = bass.ds

    assert (2 * N_TOK + N_EXP * (P - 1)) // P <= FTILES
    with ExitStack() as ctx:
        def sb(name, shape, dt):
            return ctx.enter_context(nc.sbuf_tensor(name, shape, dt))

        def sem(name):
            return ctx.enter_context(nc.semaphore(name))

        x_sb = sb("x_sb", [P, TILES, D], fp32)
        fx = sb("fx", [P, TILES, FXC], fp16)
        w1_sb = sb("w1_sb", [P, N_EXP * W1C], fp32)
        big = sb("big", [P, BIG], fp32)
        raw = big[:, 0:2 * NPAD].bitcast(i32).rearrange("p (s n) -> p s n", s=2)
        qk = big[:, 2 * NPAD:4 * NPAD].bitcast(fp16).rearrange("p (q n) -> p q n", q=4)
        mask = big[:, 4 * NPAD:6 * NPAD].bitcast(bf16).rearrange("p (s n) -> p s n", s=4)
        w2_sb = big[:, 0:N_EXP * HID]
        f32_sb = w1_sb[:, 0:NPAD].rearrange("p (t d) -> p t d", d=D)
        qk32 = w1_sb[:, NPAD:3 * NPAD].rearrange("p (t q h) -> p t q h", q=2, h=D)
        y_sb = [w1_sb[:, c * NPAD:(c + 1) * NPAD].rearrange("p (t d) -> p t d", d=D) for c in range(2)]
        p32 = sb("p32", [P, 3, 512], fp32)
        phi = sb("phi", [P, 3, 512], fp16)
        plo = sb("plo", [P, 3, 512], fp16)
        pay = sb("pay", [P, 2, 2, 2, D + 1], fp32)
        c_all = sb("c_all", [P, 2, 2, N_EXP], bf16)
        gates = sb("gates", [P, TILES, 2], fp32)
        id32 = sb("id32", [P, P], fp32)
        id16 = sb("id16", [P, P], fp16)
        idm = sb("idm", [P, P], bf16)
        tri = sb("tri", [P, P], bf16)
        ones = sb("ones", [P, P], bf16)
        wqk = sb("wqk", [P, 2 * D], fp32)
        wr = sb("wr", [P, N_EXP], fp32)
        br = sb("br", [P, N_EXP], fp32)
        b2 = sb("b2", [N_EXP, D], fp32)
        iota_e = sb("iota_e", [P, N_EXP], fp32)
        region = sb("region", [P, N_EXP], fp32)
        dest = sb("dest", [P, 2, TILES], i32)
        tok = sb("tok", [P, TILES], fp32)
        padx = sb("padx", [P, TILES], fp32)
        srow = sb("srow", [P, 1], fp32)
        sback = sb("sback", [P, 1], fp32)
        m_half = sb("m_half", [P, 2 * TILES], fp32)
        zero_e = sb("zero_e", [P, N_EXP], fp32)
        padrow = sb("padrow", [P, D + 1], fp32)
        stats = sb("stats", [P, TILES, 6], fp32)
        mean = sb("mean", [P, TILES], fp32)
        rstd = sb("rstd", [P, TILES], fp32)
        tmp = sb("tmp", [P, 4, TILES], fp32)
        ss = sb("ss", [P, TILES, 2], fp32)
        rn = sb("rn", [P, TILES, 2], fp32)
        payf = pay[:, :, :, :, :].rearrange("p a b c d -> p (a b c d)")
        sq = payf[:, 0:2 * D].rearrange("p (s n) -> p s n", s=2)
        ft = payf[:, 2 * D:4 * D].rearrange("p (s n) -> p s n", s=2)
        hl = payf[:, 4 * D:8 * D].bitcast(fp16).rearrange("p (s q n) -> p s q n", s=2, q=4)
        guard = sb("guard", [P, 2], fp32)
        den = sb("den", [P, 2, 2], fp32)
        g_sb = sb("g_sb", [P, 3, 2, D], fp32)
        v_sb = sb("v_sb", [P, 2, D], fp32)
        st2 = sb("st2", [P, 2, 6], fp32)
        mv2 = sb("mv2", [P, 2, 2], fp32)
        ve2 = sb("ve2", [P, 2], fp32)
        r2 = sb("r2", [P, 2], fp32)
        zt = sb("zt", [P, 2, P], fp32)
        lg = sb("lg", [P, 2, N_EXP], fp32)
        top = sb("top", [P, 2, 8], fp32)
        tix = sb("tix", [P, 2, 8], u32)
        tixf = sb("tixf", [P, 2, 2], fp32)
        oh = sb("oh", [P, 2, 2, N_EXP], fp32)
        ohg = sb("ohg", [P, 2, 2, N_EXP], fp32)
        comb = sb("comb", [P, 2, N_EXP], fp32)
        combt = sb("combt", [N_EXP, 2, P], fp32)
        csum = sb("csum", [P, N_EXP], bf16)
        gap = sb("gap", [P, 2], fp32)
        eg = sb("eg", [P, 2], fp32)
        eg1 = sb("eg1", [P, 2], fp32)
        place = sb("place", [P, 2, N_EXP], fp32)
        pos = sb("pos", [P, 2, 2], fp32)
        posi = sb("posi", [P, 2, 2, 2], i32)
        gf = g_sb[:, :, :, :].rearrange("p a t d -> p (a t d)")
        cnt, ntf, cin, cex, ind, ind2, junk, ends, last_row = (gf[:, n * N_EXP:(n + 1) * N_EXP] for n in range(9))
        cnti, nti = (gf[:, n * N_EXP:(n + 1) * N_EXP].bitcast(i32) for n in (9, 10))
        tv = sb("tv", [P, 4], fp32)
        table = sb("table", [1, 2 * P], i32)
        p32f = p32[:, :, :].rearrange("p r n -> p (r n)")
        xt = p32f[:, 0:2 * P].rearrange("p (s n) -> p s n", s=2)
        w1s = p32f[:, 2 * P:2 * P + 2 * W1C].rearrange("p (s n) -> p s n", s=2)
        ht = p32f[:, 6 * P + 4:10 * P + 4].rearrange("p (s h n) -> p s h n", s=2, h=2)
        rings = big[:, N_EXP * HID:]
        xg = rings[:, 0:RING * (D + 1)].rearrange("p (s n) -> p s n", s=RING)
        ys = rings[:, RING * (D + 1):RING * (2 * D + 1)].rearrange("p (s n) -> p s n", s=RING)

        def scratch(name, rows, cols):
            t = nc.dram_tensor(name, [rows, cols], fp32)
            return t.ap()

        xs = scratch("xs", XS_ROWS, D + 1)
        yt = scratch("yt", YT_ROWS, D)

        score = [ctx.enter_context(nc.psum_tensor(f"score{i}", [P, 512], fp32)) for i in range(3)]
        acc = [ctx.enter_context(nc.psum_tensor(f"acc{i}", [P, 2, 512], fp32)) for i in range(2)]
        route = ctx.enter_context(nc.psum_tensor("route", [P, 512], fp32))
        ftp = [score[0], score[1]]
        qkp = [acc[0][:, 0, :], acc[0][:, 1, :]]
        qtp = [acc[1][:, c, :].bitcast(fp16)[:, 0:512].rearrange("p (q n) -> p q n", q=4) for c in range(2)]
        xtp = [score[0], score[1]]
        hp = [[acc[0][:, 0, :], acc[0][:, 1, :]], [acc[1][:, 0, :], acc[1][:, 1, :]]]
        yp = [score[2], route]

        x_in_s = sem("x_loaded")
        w_in_s = sem("weights_loaded")
        adj_in_s = [sem(f"adj_loaded{s}") for s in range(2)]
        w1_in_s = sem("w1_loaded")
        w2_in_s = sem("w2_loaded")
        const_s = sem("constants_made")
        chain_s = sem("dve_step")
        pchain_s = sem("pool_step")
        pstep_s = sem("pool_route_step")
        bn_s = sem("x_row_stats")
        hi_s = sem("high_parts_made")
        half_s = sem("first_choice_added")
        st2_s = sem("x1_row_stats")
        lgb_s = sem("logits_biased")
        ypad_s = sem("y_padding_made")
        stats_s = sem("stats_made")
        rstd_s = sem("rstd_made")
        f_s = sem("f_made")
        fx_s = sem("fx_made")
        ftp_s = sem("f_transposed")
        ft_s = sem("f_transposed_copied")
        qk_s = sem("qk_projected")
        qk32_s = sem("qk_copied")
        ss_s = sem("squares_summed")
        rn_s = sem("row_norms_made")
        hl_s = sem("qk_split")
        qt_s = sem("qk_transposed")
        qtc_s = sem("qk_transposed_copied")
        mask_s = sem("mask_made")
        score_s = sem("scores_made")
        exp_s = sem("exponentials_made")
        lo_s = sem("low_parts_made")
        pv_s = sem("pair_accumulated")
        den_s = sem("guards_made")
        u_s = sem("residual_made")
        accread_s = sem("accumulators_read")
        mv_s = sem("moments_made")
        r2_s = sem("rstd2_made")
        z_s = sem("z_made")
        pay_s = sem("payload_made")
        ztp_s = sem("z_transposed")
        zt_s = sem("z_transposed_copied")
        lg_s = sem("logits_made")
        cho_s = sem("choices_made")
        eg_s = sem("gate_exponentials_made")
        cmb_s = sem("combine_made")
        rank_s = sem("ranks_made")
        pos_s = sem("positions_made")
        cbt_s = sem("combine_transposed")
        cbc_s = sem("combine_transposed_copied")
        b2_s = sem("b2_share_made")
        b2a_s = sem("b2_share_added")
        scat_s = [sem(f"rows_scattered{c}") for c in range(2)]
        cnt_s = sem("counts_made")
        tv_s = sem("table_columns_made")
        tr_s = sem("table_rows_made")
        tab_s = sem("table_made")
        padw_s = sem("padding_written")
        xg_s = [sem(f"tile_loaded{c}") for c in range(RING)]
        xtp_s = sem("tile_transposed")
        xt_s = sem("tile_transposed_copied")
        w1s_s = sem("w1_picked")
        hp_s = sem("hidden_made")
        h0_s = sem("hidden0_activated")
        h1_s = sem("hidden1_activated")
        yp_s = sem("results_made")
        ys_s = [sem(f"results_copied{c}") for c in range(RING)]
        ysc_s = [sem(f"results_scattered{c}") for c in range(RING)]
        y_in_s = [sem(f"y_loaded{c}") for c in range(len(CHUNKS))]
        out_s = sem("combined")
        st_s = sem("stored")

        def slot(b_odd, k):
            return (k + b_odd) % 3

        def since(b_odd, k):
            n = 1
            while True:
                q = k - n
                odd = b_odd if q >= 0 else 1 - b_odd
                if slot(odd, q % PAIRS) == slot(b_odd, k):
                    return n
                n += 1

        def at_once(eng):
            eng.wait_ge(const_s, 1)

        def expert_tiles(eng, turn):
            turn(0, RING)
            with eng.Fori(1, TURNS) as it:
                turn(it, RING)
            turn(TURNS, REST)

        def wait_scattered(eng, it, c):
            if not isinstance(it, int) or it > 0:
                eng.wait_ge(ysc_s[c], it * 16)

        def entry_registers(eng, name):
            return [eng.alloc_register(f"{name}{c}") for c in range(RING)]

        def load_entries(eng, regs, col, n, top):
            eng.load(regs[:n], table[0:1, ds(col, n)])
            return [eng.snap(r, min_val=0, max_val=top) for r in regs[:n]]

        block = ctx.enter_context(nc.Block())

        @block.sync
        def _(sp):
            for c in range(2):
                half = slice(c * (TILES // 2), (c + 1) * (TILES // 2))
                sp.dma_start(x_sb[:, half, :], x_in[:, half, :]).then_inc(x_in_s, 16)

            def load_adj(t, s):
                sp.dma_start(raw[:, s, :], adj_in[ds(t * P, P), :]).then_inc(adj_in_s[s], 16)

            for s in range(2):
                load_adj(s, s)
            sp.wait_ge(const_s, 1)
            sp.dma_start(xs.rearrange("(e r) d -> r e d", r=CAP)[0:P], padrow[:, None, :].to_broadcast([P, N_EXP, D + 1]))\
              .then_inc(padw_s, 16)
            W1P = N_EXP * W1C // 8
            with sp.Fori(1, 9) as b:
                for s in range(2):
                    sp.wait_ge(mask_s, b * 2 + (s - 1))
                    load_adj(b * 2 + s, s)
                sp.wait_ge(qtc_s, TILES + 2)
                sp.wait_ge(fx_s, 1)
                sp.dma_start(w1_sb[:, ds((b - 1) * W1P, W1P)], w1_in[:, ds((b - 1) * W1P, W1P)])\
                  .then_inc(w1_in_s, 16)
            with sp.Fori(9, BLOCKS) as b:
                for s in range(2):
                    sp.wait_ge(mask_s, b * 2 + (s - 1))
                    load_adj(b * 2 + s, s)
            sp.wait_ge(mask_s, TILES)
            cut = 2 * NPAD
            sp.dma_start(w2_sb[:, 0:cut], w2_in[:, 0:cut]).then_inc(w2_in_s, 16)
            sp.wait_ge(pv_s, BLOCKS * PAIRS + 3)
            sp.dma_start(w2_sb[:, cut:N_EXP * HID], w2_in[:, cut:N_EXP * HID]).then_inc(w2_in_s, 16)
            sp.wait_ge(tab_s, 1)
            for c in range(2):
                sp.wait_ge(scat_s[c], 64 * (BLOCKS // 2 + (1 - c)))
            row_regs = entry_registers(sp, "row")

            def load_turn(it, n):
                for c0 in range(0, n, 4):
                    rows = load_entries(sp, row_regs[c0:], it * RING + (P + c0), 4, XS_ROWS - P)
                    for c in range(c0, c0 + 4):
                        wait_scattered(sp, it, c)
                        sp.dma_start(xg[:, c, :], xs[ds(rows[c - c0], P), :]).then_inc(xg_s[c], 16)

            expert_tiles(sp, load_turn)
            for c in range(RING):
                sp.wait_ge(ysc_s[c], (TURNS + (c < REST)) * 16)
            sp.wait_ge(ypad_s, 1)
            for h, (t0, t1) in enumerate(CHUNKS):
                whole = min(t1, TILES - 1)
                for c in range(2):
                    src = yt[c * NPAD:(c + 1) * NPAD, :].rearrange("(t p) d -> p t d", p=P)
                    sp.dma_start(y_sb[c][:, t0:whole, :], src[:, t0:whole, :]).then_inc(y_in_s[h], 16)
                    if t1 == TILES:
                        sp.dma_start(y_sb[c][0:112, t1 - 1, :], src[0:112, t1 - 1, :]).then_inc(y_in_s[h], 16)
                        sp.dma_start(y_sb[c][112:127, t1 - 1, :], src[112:127, t1 - 1, :]).then_inc(y_in_s[h], 16)
            for t0, t1 in CHUNKS:
                sp.wait_ge(out_s, t1)
                sp.dma_start(out[:, t0:t1, :], x_sb[:, t0:t1, :]).then_inc(st_s, 16)
            sp.wait_ge(st_s, 16 * len(CHUNKS))

        @block.gpsimd
        def _(pool):
            count = [0]

            def link(ins):
                count[0] += 1
                ins.then_inc(pchain_s, 1)
                pool.wait_ge(pchain_s, count[0])

            link(pool.memset(m_half[:, :], -0.5))
            for m in (id32, id16, idm):
                link(pool.memset(m[:, :], 0.0))
                link(pool.affine_select(out=m[:, :], in_=m[:, :], compare_op=ALU.not_equal,
                                        fill=32768.0 if m is idm else 1.0,
                                        base=0, pattern=[[-1, P]], channel_multiplier=1))
            link(pool.memset(ones[:, :], 1.0))
            link(pool.affine_select(out=tri[:, :], in_=ones[:, :], compare_op=ALU.is_gt, fill=0.0,
                                    base=0, pattern=[[1, P]], channel_multiplier=-1))
            link(pool.memset(csum[:, :], 0.0))
            link(pool.memset(zero_e[:, :], 0.0))
            link(pool.memset(padrow[:, :], 0.0))
            link(pool.iota(iota_e[:, :], [[1, N_EXP]], base=0, channel_multiplier=0,
                           allow_small_or_imprecise_dtypes=True))
            link(pool.iota(dest[:, :, :], [[NPAD, 2], [P, TILES]], base=0, channel_multiplier=1))
            link(pool.iota(tok[:, :], [[P, TILES]], base=0, channel_multiplier=1,
                           allow_small_or_imprecise_dtypes=True))
            link(pool.iota(srow[:, :], [[0, 1]], base=0, channel_multiplier=1,
                           allow_small_or_imprecise_dtypes=True))
            link(pool.iota(padrow[:, D:D + 1].bitcast(i32), [[0, 1]], base=NOWHERE, channel_multiplier=0))
            link(pool.tensor_scalar(region[:, :], iota_e[:, :], float(CAP), float(P), ALU.mult, ALU.add))
            link(pool.tensor_scalar(padx[:, :], tok[:, :], float(N_TOK), float(NOWHERE), ALU.is_ge, ALU.mult))
            pool.tensor_scalar(sback[:, :], srow[:, :], -float(P), -float(P), ALU.mult, ALU.add)\
                .then_inc(const_s, 1)

            pool.wait_ge(stats_s, 1)
            link(pool.tensor_scalar(tmp[:, 3, :], tmp[:, 2, :], EPS, None, ALU.add))
            pool.tensor_tensor(rstd[:, :], tmp[:, 3, :], m_half[:, 0:TILES], ALU.pow).then_inc(rstd_s, 1)

            pool.wait_ge(ss_s, 2 * TILES + 1)
            rn_flat = rn[:, :, :].rearrange("p t q -> p (t q)")
            ss_flat = ss[:, :, :].rearrange("p t q -> p (t q)")
            link(pool.tensor_scalar(ss_flat, ss_flat, 1e-8, None, ALU.max))
            pool.tensor_tensor(rn_flat, ss_flat, m_half[:, :], ALU.pow).then_inc(rn_s, 1)

            def residual(e, odd):
                fx2 = fx[:, ds(e * 2, 2), :]
                pool.wait_ge(fx_s, 1)
                pool.tensor_tensor(g_sb[:, 0], fx2[:, :, 0:D], fx2[:, :, D:2 * D], ALU.add).then_inc(pstep_s, 1)
                pool.wait_ge(den_s, e + 1)
                pool.wait_ge(pstep_s, e * 4 + 1)
                pool.tensor_tensor(g_sb[:, 1], g_sb[:, 0], guard[:, :, None].to_broadcast([P, 2, D]), ALU.mult)\
                    .then_inc(pstep_s, 1)
                pool.wait_ge(pstep_s, e * 4 + 2)
                pool.tensor_tensor(g_sb[:, 2], g_sb[:, 1], x_sb[:, ds(e * 2, 2), :], ALU.add).then_inc(u_s, 1)

            def second_norm(e, odd):
                at_once(pool)
                pool.wait_ge(mv_s, e + 1)
                pool.tensor_scalar(ve2[:, :], mv2[:, :, 1], EPS, None, ALU.add).then_inc(pstep_s, 1)
                pool.wait_ge(pstep_s, e * 4 + 3)
                pool.tensor_tensor(r2[:, :], ve2[:, :], m_half[:, 0:2], ALU.pow).then_inc(r2_s, 1)

            def payload(e, odd):
                pool.tensor_copy(pay[:, odd, :, :, D:D + 1].bitcast(i32),
                                 dest[:, :, ds(e * 2, 2)].rearrange("p c t -> p t c")[:, :, :, None])\
                    .then_inc(pstep_s, 1)
                at_once(pool)
                pool.wait_ge(z_s, e + 1)
                pool.tensor_copy(pay[:, odd, :, 1, 0:D], pay[:, odd, :, 0, 0:D]).then_inc(pay_s, 1)

            def scatters(e, odd):
                at_once(pool)
                pool.wait_ge(pos_s, e + 1)
                pool.wait_ge(pay_s, e + 1)
                for t in range(2):
                    for c in range(2):
                        pool.indirect_dma_start(
                            out=xs[:, :], out_offset=bass.IndirectOffsetOnAxis(ap=posi[:, odd, t, c:c + 1], axis=0),
                            in_=pay[:, odd, t, c, :], in_offset=None,
                            bounds_check=XS_ROWS - 1, oob_is_err=False).then_inc(scat_s[odd], 16)

            pool.wait_ge(const_s, 1)
            pool.wait_ge(padw_s, 16)

            def body(e, odd, again=True):
                residual(e, odd)
                second_norm(e, odd)
                at_once(pool)
                if again:
                    pool.wait_ge(scat_s[odd], (e - odd) * 32)
                payload(e, odd)
                scatters(e, odd)

            body(0, 0, again=False)
            body(1, 1, again=False)
            with pool.Fori(1, (BLOCKS - 1) // 2) as it:
                for u in range(2):
                    body(it * 2 + u, u)
            body(BLOCKS - 1, 0)

            def send_turn(nth, n):
                for c in range(n):
                    at_once(pool)
                    pool.wait_ge(ys_s[c], nth)
                    pool.indirect_dma_start(
                        out=yt[:, :], out_offset=bass.IndirectOffsetOnAxis(ap=xg[:, c, D:D + 1].bitcast(i32), axis=0),
                        in_=ys[:, c, :], in_offset=None, bounds_check=YT_ROWS - 1, oob_is_err=False)\
                        .then_inc(ysc_s[c], 16)

            with pool.Fori(1, TURNS + 1) as nth:
                send_turn(nth, RING)
            send_turn(TURNS + 1, REST)

        @block.tensor
        def _(pe):
            mm = nc.tensor.matmul
            pe.sem_inc(qk_s, 2)
            pe.sem_inc(qt_s, 2)
            pe.wait_ge(const_s, 1)
            pe.wait_ge(w_in_s, 64)

            def project(t, u):
                pe.wait_ge(ft_s, t + 3)
                pe.wait_ge(qk32_s, t + 1)
                mm(qkp[u][:, 0:2 * D], ft[:, u, :], wqk[:, :], start=True, stop=True).then_inc(qk_s, 1)

            for it in range(TILES // 2):
                for u in range(2):
                    pe.wait_ge(f_s, it * 2 + u + 1)
                    pe.wait_ge(ft_s, it * 2 + u + 1)
                    nc.tensor.transpose(ftp[u][:, 0:P], f32_sb[:, it * 2 + u, :], id32[:, :]).then_inc(ftp_s, 1)
                for u in range(2):
                    project(it * 2 + u, u)
            with pe.Fori(0, TILES // 2) as it:
                for u in range(2):
                    pe.wait_ge(hl_s, it * 2 + (u + 1))
                    pe.wait_ge(qtc_s, it * 2 + (u + 1))
                    for q in range(4):
                        last = nc.tensor.transpose(qtp[u][:, q, :], hl[:, u, q, :], id16[:, :])
                    last.then_inc(qt_s, 1)

            def scores(b, odd, k):
                p = b * PAIRS + k
                r = slot(odd, k)
                if k == 0:
                    pe.wait_ge(mask_s, b * 2 + 2)
                pe.wait_ge(exp_s, p - since(odd, k) + 4)
                for j in range(2):
                    o = score[r][:, 256 * j:256 * j + 256]
                    cols = slice((2 * k + j) * P, (2 * k + j + 1) * P)
                    for i in range(2):
                        mm(o[:, P * i:P * i + P], mask[:, 2 * odd + i, cols], idm[:, :],
                           start=(j == 0 and i == 0), stop=False, skip_group_check=True)
                    for n, (a, c) in enumerate(((0, 2), (0, 3), (1, 2))):
                        last = mm(o, qk[:, a, cols], qk[:, c, ds(b * 256, 256)],
                                  start=False, stop=(n == 2 and j == 1), skip_group_check=True)
                last.then_inc(score_s, 1)

            def accumulate(b, odd, k):
                p = b * PAIRS + k
                r = slot(odd, k)
                if k == 0 and not (isinstance(b, int) and b < 2):
                    pe.wait_ge(accread_s, b - 1)
                pe.wait_ge(lo_s, p + 1)
                for j in range(2):
                    t = 2 * k + j
                    for i in range(2):
                        w = slice(256 * j + P * i, 256 * j + P * i + P)
                        mm(acc[odd][:, i, 0:FXC], phi[:, r, w], fx[:, t, :],
                           start=(t == 0), stop=False, skip_group_check=True)
                        last = mm(acc[odd][:, i, D:FXC], plo[:, r, w], fx[:, t, D:FXC],
                                  start=False, stop=(t == TILES - 1), skip_group_check=True)
                last.then_inc(pv_s, 1)

            def route_zt(e, odd):
                pe.wait_ge(z_s, e + 1)
                pe.wait_ge(b2a_s, e)
                for t in range(2):
                    last = nc.tensor.transpose(route[:, P * t:P * t + P], pay[:, odd, t, 0, 0:D], id32[:, :])
                last.then_inc(ztp_s, 1)

            def route_logits(e):
                pe.wait_ge(zt_s, e + 1)
                for t in range(2):
                    last = mm(route[:, 256 + 64 * t:320 + 64 * t], zt[:, t, :], wr[:, :], start=True, stop=True)
                last.then_inc(lg_s, 1)

            def route_ranks(e, odd):
                pe.wait_ge(cho_s, e + 1)
                for t in range(2):
                    o = route[:, 384 + 64 * t:448 + 64 * t]
                    mm(o, tri[:, :], c_all[:, odd, t, :], start=True, stop=False)
                    last = mm(o, ones[:, :], csum[:, :], start=False, stop=(t == 0))
                    if t == 1:
                        last = mm(o, ones[:, :], c_all[:, odd, 0, :], start=False, stop=True)
                last.then_inc(rank_s, 1)

            def route_combine(e):
                at_once(pe)
                pe.wait_ge(cmb_s, e + 1)
                pe.wait_ge(pos_s, e + 1)
                for t in range(2):
                    last = nc.tensor.transpose(route[0:N_EXP, P * t:P * t + P], comb[:, t, :], id32[:, :])
                last.then_inc(cbt_s, 1)

            def route_b2(e):
                pe.wait_ge(cbc_s, e + 1)
                for t in range(2):
                    last = mm(route[:, 256 + P * t:384 + P * t], combt[:, t, :], b2[:, :], start=True, stop=True)
                last.then_inc(b2_s, 1)

            def route_step(e, odd, k):
                if k == 4:
                    route_zt(e, odd)
                if k == 6:
                    route_logits(e)
                if k == 8:
                    route_ranks(e, odd)
                if k == 11:
                    route_combine(e)

            pe.wait_ge(qtc_s, TILES + 2)
            pe.wait_ge(fx_s, 1)
            scores(0, 0, 0)
            scores(0, 0, 1)

            def body(b, odd, routed=True, late=True, ahead=True):
                for k in range(PAIRS):
                    if k + 2 < PAIRS:
                        scores(b, odd, k + 2)
                    elif ahead:
                        scores(b + 1, 1 - odd, k + 2 - PAIRS)
                    accumulate(b, odd, k)
                    if late and k == 1:
                        route_b2(b - 2)
                    if routed:
                        route_step(b - 1, 1 - odd, k)

            body(0, 0, routed=False, late=False)
            body(1, 1, late=False)
            with pe.Fori(1, (BLOCKS - 1) // 2) as it:
                for u in range(2):
                    body(it * 2 + u, u)
            body(BLOCKS - 1, 0, ahead=False)
            route_b2(BLOCKS - 2)
            for k in range(PAIRS):
                route_step(BLOCKS - 1, 0, k)
            route_b2(BLOCKS - 1)
            pe.wait_ge(b2a_s, BLOCKS)
            mm(route[:, 0:N_EXP], ones[:, :], csum[:, :], start=True, stop=True).then_inc(cnt_s, 1)
            pe.wait_ge(tv_s, 1)
            for c in range(2):
                last = mm(route[0:1, P * c:P * c + P], tv[:, c:c + 1], id32[:, :], start=True, stop=True)
            last.then_inc(tr_s, 1)
            pe.wait_ge(tab_s, 1)
            pe.wait_ge(w2_in_s, 32)

            def transpose_tile(it, c):
                pe.wait_ge(xg_s[c], it * 16 + 16)
                pe.wait_ge(xt_s, it * RING + (c + 1))
                nc.tensor.transpose(xtp[c % 2][:, 0:P], xg[:, c, 0:D], id32[:, :]).then_inc(xtp_s, 1)

            def hidden(it, c):
                pe.wait_ge(xt_s, it * RING + (c + 3))
                pe.wait_ge(w1s_s, it * RING + (c + 1))
                pe.wait_ge(h0_s, it * RING + (c + 1))
                pe.wait_ge(h1_s, it * RING + (c + 1))
                for h in range(2):
                    last = mm(hp[c % 2][h][:, 0:P], w1s[:, c % 2, P * h:P * h + P], xt[:, c % 2, :],
                              start=True, stop=True)
                last.then_inc(hp_s, 1)

            def results(it, c, e):
                pe.wait_ge(h0_s, it * RING + (c + 3))
                pe.wait_ge(h1_s, it * RING + (c + 3))
                if c >= 2:
                    pe.wait_ge(ys_s[c - 2], it + 1)
                elif not isinstance(it, int) or it > 0:
                    pe.wait_ge(ys_s[c - 2 + RING], it)
                for h in range(2):
                    last = mm(yp[c % 2][:, 0:D], ht[:, c % 2, h, :], w2_sb[:, ds(e * HID + P * h, P)],
                              start=(h == 0), stop=(h == 1))
                last.then_inc(yp_s, 1)

            expert_regs = entry_registers(pe, "w2_expert")
            transpose_tile(0, 0)
            transpose_tile(0, 1)
            hidden(0, 0)

            def tiles_turn(it, n):
                experts = load_entries(pe, expert_regs, it * RING, n, N_EXP - 1)
                for c in range(n):
                    for ahead, stage in ((2, transpose_tile), (1, hidden)):
                        if n == RING or c + ahead < n:
                            stage(it + (c + ahead) // RING, (c + ahead) % RING)
                    results(it, c, experts[c])

            expert_tiles(pe, tiles_turn)

        @block.scalar
        def _(act):
            A = nc.scalar.activation
            act.dma_start(wqk[:, :], wqk_in[:, :]).then_inc(w_in_s, 16)
            act.dma_start(wr[:, :], wr_in[:, :]).then_inc(w_in_s, 16)
            act.dma_start(br[:, :], br_in[:, :]).then_inc(w_in_s, 16)
            act.dma_start(b2[:, :], b2_in[:, :]).then_inc(w_in_s, 16)
            act.sem_inc(ft_s, 2)
            act.sem_inc(qtc_s, 2)
            act.sem_inc(exp_s, 3)
            act.sem_inc(ss_s, 1)
            act.sem_inc(xt_s, 2)
            act.sem_inc(h0_s, 2)

            with act.Fori(0, TILES // 2) as it:
                for u in range(2):
                    act.wait_ge(ftp_s, it * 2 + (u + 1))
                    act.wait_ge(qk_s, it * 2 + (u + 1))
                    A(ft[:, u, :], ftp[u][:, 0:P], ACT.Copy).then_inc(ft_s, 1)
                for u in range(2):
                    act.wait_ge(qk32_s, it * 2 + (u + 3))
                    for q in range(2):
                        act.wait_ge(ss_s, it * 4 + (2 * u + q + 1))
                        A(sq[:, 1, :], qk32[:, ds(it * 2 + u, 1), q, :], ACT.Square,
                          accum_out=ss[:, ds(it * 2 + u, 1), q]).then_inc(ss_s, 1)
            with act.Fori(0, TILES // 2) as it:
                for u in range(2):
                    act.wait_ge(qt_s, it * 2 + (u + 3))
                    A(qk[:, :, ds(it * 256 + P * u, P)], qtp[u], ACT.Copy).then_inc(qtc_s, 1)

            def exps(b, odd, k):
                p = b * PAIRS + k
                r = slot(odd, k)
                act.wait_ge(score_s, p + 1)
                act.wait_ge(pv_s, p - since(odd, k) + 4)
                A(p32[:, r, :], score[r][:, :], ACT.Exp)
                A(phi[:, r, :], score[r][:, :], ACT.Exp).then_inc(exp_s, 1)

            def route_step(e, k):
                if k == 6:
                    act.wait_ge(ztp_s, e + 1)
                    A(zt[:, :, :], route[:, 0:256].rearrange("p (t n) -> p t n", t=2), ACT.Copy).then_inc(zt_s, 1)
                if k == 10:
                    act.wait_ge(cho_s, e + 1)
                    A(eg[:, :], gap[:, :], ACT.Exp).then_inc(eg_s, 1)

            def body(b, odd, routed=True):
                for k in range(PAIRS):
                    exps(b, odd, k)
                    if routed:
                        route_step(b - 1, k)

            body(0, 0, routed=False)
            body(1, 1)
            with act.Fori(1, (BLOCKS - 1) // 2) as it:
                for u in range(2):
                    body(it * 2 + u, u)
            body(BLOCKS - 1, 0)
            for k in range(PAIRS):
                route_step(BLOCKS - 1, k)

            def tile_in(it, c):
                act.wait_ge(xtp_s, it * RING + (c + 1))
                act.wait_ge(hp_s, it * RING + (c + 1))
                A(xt[:, c % 2, :], xtp[c % 2][:, 0:P], ACT.Copy).then_inc(xt_s, 1)

            def relu(it, c):
                act.wait_ge(hp_s, it * RING + (c + 3))
                act.wait_ge(yp_s, it * RING + (c + 1))
                A(ht[:, c % 2, 0, :], hp[c % 2][0][:, 0:P], ACT.Relu, bias=w1s[:, c % 2, HID:HID + 1])\
                    .then_inc(h0_s, 1)

            def result(it, c):
                act.wait_ge(yp_s, it * RING + (c + 3))
                wait_scattered(act, it, c)
                A(ys[:, c, :], yp[c % 2][:, 0:D], ACT.Copy).then_inc(ys_s[c], 1)

            tile_in(0, 0)
            tile_in(0, 1)
            relu(0, 0)

            def tiles_turn(it, n):
                for c in range(n):
                    for ahead, stage in ((2, tile_in), (1, relu)):
                        if n == RING or c + ahead < n:
                            stage(it + (c + ahead) // RING, (c + ahead) % RING)
                    result(it, c)

            expert_tiles(act, tiles_turn)

        @block.vector
        def _(dve):
            V = nc.vector
            count = [0, 0]

            def link(ins):
                count[0] += 1
                ins.then_inc(chain_s, 1)
                dve.wait_ge(chain_s, count[1] + count[0])

            dve.sem_inc(qk32_s, 2)
            dve.sem_inc(pv_s, 3)
            for credit in (h1_s, hp_s, yp_s):
                dve.sem_inc(credit, 2)
            V.memset(fx[:, :, 2 * D:FXC], 1.0)

            dve.wait_ge(x_in_s, 32)
            for c in range(2):
                with dve.Fori(13 * c, 13 * (c + 1)) as t:
                    V.bn_stats(stats[:, ds(t, 1), :], x_sb[:, ds(t, 1), :]).then_inc(bn_s, 1)
            dve.wait_ge(bn_s, TILES)
            even, odd_m = stats[:, :, 1], stats[:, :, 4]
            link(V.tensor_tensor(tmp[:, 0, :], even, odd_m, ALU.add))
            link(V.tensor_scalar(mean[:, :], tmp[:, 0, :], 0.5, None, ALU.mult))
            link(V.tensor_tensor(tmp[:, 1, :], even, odd_m, ALU.subtract))
            link(V.scalar_tensor_tensor(tmp[:, 0, :], tmp[:, 1, :], 0.25, tmp[:, 1, :], ALU.mult, ALU.mult))
            link(V.tensor_tensor(tmp[:, 1, :], stats[:, :, 2], stats[:, :, 5], ALU.add))
            V.scalar_tensor_tensor(tmp[:, 2, :], tmp[:, 1, :], 1.0 / D, tmp[:, 0, :], ALU.mult, ALU.add)\
             .then_inc(stats_s, 1)
            dve.wait_ge(rstd_s, 1)
            with dve.Fori(0, TILES) as t:
                V.tensor_scalar(f32_sb[:, ds(t, 1), :], x_sb[:, ds(t, 1), :], mean[:, ds(t, 1)], rstd[:, ds(t, 1)],
                                ALU.subtract, ALU.mult).then_inc(f_s, 1)
            with dve.Fori(0, TILES // 2) as it:
                for u in range(2):
                    dve.wait_ge(qk_s, it * 2 + (u + 3))
                    V.tensor_copy(qk32[:, ds(it * 2 + u, 1), :, :],
                                  qkp[u][:, 0:2 * D].rearrange("p (q h) -> p q h", q=2)).then_inc(qk32_s, 1)
            link(V.tensor_copy(fx[:, :, D:2 * D], f32_sb[:, :, :]))
            V.tensor_tensor(fx[:, :, 0:D], f32_sb[:, :, :], fx[:, :, D:2 * D], ALU.subtract).then_inc(fx_s, 1)

            def convert(t, slot_, s, part, parts):
                w = NPAD // parts
                cols = slice(part * w, (part + 1) * w)
                if part == 0:
                    dve.wait_ge(adj_in_s[s], (t - s) * 8 + 16)
                return V.tensor_scalar(mask[:, slot_, cols], raw[:, s, cols], 0.0, 1.0, ALU.is_gt, ALU.subtract)

            for s in range(2):
                convert(s, s, s, 0, 1).then_inc(mask_s, 1)
            dve.wait_ge(rn_s, 1)
            with dve.Fori(0, TILES // 2) as it:
                for u in range(2):
                    dve.wait_ge(qt_s, it * 2 + (u + 1))
                    for q in range(2):
                        V.tensor_scalar(hl[:, u, 2 * q, :], qk32[:, ds(it * 2 + u, 1), q, :],
                                        rn[:, ds(it * 2 + u, 1), q], None, ALU.mult).then_inc(hi_s, 1)
                    for q in range(2):
                        dve.wait_ge(hi_s, it * 4 + (2 * u + q + 1))
                        last = V.scalar_tensor_tensor(hl[:, u, 2 * q + 1, :], qk32[:, ds(it * 2 + u, 1), q, :],
                                                      rn[:, ds(it * 2 + u, 1), q], hl[:, u, 2 * q, :],
                                                      ALU.mult, ALU.subtract)
                    last.then_inc(hl_s, 1)

            dve.wait_ge(const_s, 1)
            dve.wait_ge(w_in_s, 64)

            def low(b, odd, k):
                p = b * PAIRS + k
                r = slot(odd, k)
                dve.wait_ge(exp_s, p + 4)
                V.tensor_tensor(plo[:, r, :], p32[:, r, :], phi[:, r, :], ALU.subtract).then_inc(lo_s, 1)

            def route_step(e, odd, k):
                a = acc[odd]
                tiles = ds(e * 2, 2)
                if k == 0:
                    dve.wait_ge(pv_s, e * PAIRS + (PAIRS + 3))
                    link(V.tensor_scalar(den[:, 0, :], a[:, :, 2 * D], 0.0, 0.5, ALU.is_le, ALU.mult))
                    V.tensor_scalar(guard[:, :], den[:, 0, :], 0.5, None, ALU.add).then_inc(den_s, 1)
                    link(V.tensor_scalar(den[:, 1, :], a[:, :, 2 * D], 1e-30, 2.0, ALU.max, ALU.mult))
                    link(V.reciprocal(den[:, 0, :], den[:, 1, :]))
                if k == 2:
                    dve.wait_ge(u_s, e + 1)
                    for t in range(2):
                        last = V.scalar_tensor_tensor(v_sb[:, t, :], a[:, t, 0:D], den[:, 0, t:t + 1],
                                                      g_sb[:, 2, t, :], ALU.mult, ALU.add)
                    link(last)
                    for t in range(2):
                        last = V.scalar_tensor_tensor(x_sb[:, ds(e * 2 + t, 1), :].rearrange("p o d -> p (o d)"),
                                                      a[:, t, D:2 * D], den[:, 0, t:t + 1],
                                                      v_sb[:, t, :], ALU.mult, ALU.add)
                    last.then_inc(accread_s, 1)
                    at_once(dve)
                    dve.wait_ge(accread_s, e + 1)
                    for t in range(2):
                        last = V.bn_stats(st2[:, t, :], x_sb[:, ds(e * 2 + t, 1), :])
                    last.then_inc(st2_s, 1)
                    at_once(dve)
                    dve.wait_ge(st2_s, e + 1)
                    for t in range(2):
                        last = V.bn_aggr(mv2[:, t, :], st2[:, t, :])
                    last.then_inc(mv_s, 1)
                if k == 4:
                    dve.wait_ge(r2_s, e + 1)
                    dve.wait_ge(pstep_s, e * 4 + 4)
                    for t in range(2):
                        last = V.tensor_scalar(pay[:, odd, t, 0, 0:D],
                                               x_sb[:, ds(e * 2 + t, 1), :],
                                               mv2[:, t, 0:1], r2[:, t:t + 1], ALU.subtract, ALU.mult)
                    last.then_inc(z_s, 1)
                if k == 8:
                    dve.wait_ge(lg_s, e + 1)
                    V.tensor_tensor(lg[:, :, :], route[:, 256:384].rearrange("p (t n) -> p t n", t=2),
                                    br[:, None, :].to_broadcast([P, 2, N_EXP]), ALU.add).then_inc(lgb_s, 1)
                    at_once(dve)
                    dve.wait_ge(lgb_s, e + 1)
                    for t in range(2):
                        last = V.max(top[:, t, :], lg[:, t, :])
                    link(last)
                    V.tensor_tensor(gap[:, :], top[:, :, 1], top[:, :, 0], ALU.subtract)
                    for t in range(2):
                        last = V.max_index(tix[:, t, :], top[:, t, :], lg[:, t, :])
                    link(last)
                    link(V.tensor_tensor(tixf[:, :, :], tix[:, :, 0:2],
                                         padx[:, tiles][:, :, None].to_broadcast([P, 2, 2]), ALU.add))
                    link(V.tensor_tensor(oh[:, :, :, :], iota_e[:, None, None, :].to_broadcast([P, 2, 2, N_EXP]),
                                         tixf[:, :, :, None].to_broadcast([P, 2, 2, N_EXP]), ALU.is_equal))
                    V.tensor_tensor(c_all[:, odd, :, :], oh[:, :, 0, :], oh[:, :, 1, :], ALU.add).then_inc(cho_s, 1)
                if k == 10:
                    dve.wait_ge(eg_s, e + 1)
                    link(V.tensor_scalar(eg1[:, :], eg[:, :], 1.0, None, ALU.add))
                    link(V.reciprocal(gates[:, tiles, 0], eg1[:, :]))
                    link(V.tensor_tensor(gates[:, tiles, 1], eg[:, :], gates[:, tiles, 0], ALU.mult))
                    link(V.tensor_tensor(ohg[:, :, :, :], oh[:, :, :, :],
                                         gates[:, tiles, :][:, :, :, None].to_broadcast([P, 2, 2, N_EXP]), ALU.mult))
                    V.tensor_tensor(comb[:, :, :], ohg[:, :, 0, :], ohg[:, :, 1, :], ALU.add).then_inc(cmb_s, 1)
                if k == 11:
                    dve.wait_ge(rank_s, e + 1)
                    link(V.tensor_tensor(place[:, :, :], route[:, 384:512].rearrange("p (t n) -> p t n", t=2),
                                         region[:, None, :].to_broadcast([P, 2, N_EXP]), ALU.add))
                    dve.wait_ge(cmb_s, e + 1)
                    link(V.tensor_tensor(ohg[:, :, :, :], oh[:, :, :, :],
                                         place[:, :, None, :].to_broadcast([P, 2, 2, N_EXP]), ALU.mult))
                    link(V.tensor_reduce(pos[:, :, :], ohg[:, :, :, :], AX.X, ALU.add))
                    V.tensor_tensor(posi[:, odd, :, :], pos[:, :, :],
                                    padx[:, tiles][:, :, None].to_broadcast([P, 2, 2]), ALU.add).then_inc(pos_s, 1)
                    link(V.tensor_tensor(csum[:, :], csum[:, :], c_all[:, odd, 0, :], ALU.add))
                    link(V.tensor_tensor(csum[:, :], csum[:, :], c_all[:, odd, 1, :], ALU.add))

            def combine_copy(e):
                dve.wait_ge(cbt_s, e + 1)
                V.tensor_copy(combt[:, :, :], route[0:N_EXP, 0:256].rearrange("p (t n) -> p t n", t=2))\
                 .then_inc(cbc_s, 1)

            def b2_add(e):
                dve.wait_ge(b2_s, e + 1)
                V.tensor_tensor(x_sb[:, ds(e * 2, 2), :], x_sb[:, ds(e * 2, 2), :],
                                route[:, 256:512].rearrange("p (t n) -> p t n", t=2), ALU.add).then_inc(b2a_s, 1)

            def body(b, odd, routed=True, late=True, conv=True):
                for k in range(PAIRS):
                    low(b, odd, k)
                    if late and k == 0:
                        combine_copy(b - 2)
                    if late and k == 3:
                        b2_add(b - 2)
                    if routed:
                        route_step(b - 1, 1 - odd, k)
                    if conv and k in (3, 5, 6, 7):
                        n = (3, 5, 6, 7).index(k)
                        c = convert(b * 2 + (2 + n // 2), 2 * (1 - odd) + n // 2, n // 2, n % 2, 2)
                        if n % 2:
                            c.then_inc(mask_s, 1)

            body(0, 0, routed=False, late=False)
            body(1, 1, late=False)
            start = count[0]
            with dve.Fori(1, (BLOCKS - 1) // 2) as it:
                count[1] = (it - 1) * LOOP_LINKS
                for u in range(2):
                    body(it * 2 + u, u)
            assert count[0] - start == LOOP_LINKS, count[0] - start
            count[1] = 0
            count[0] = start + ((BLOCKS - 1) // 2 - 1) * LOOP_LINKS
            body(BLOCKS - 1, 0, conv=False)
            combine_copy(BLOCKS - 2)
            b2_add(BLOCKS - 2)
            for k in range(PAIRS):
                route_step(BLOCKS - 1, 0, k)
            combine_copy(BLOCKS - 1)
            b2_add(BLOCKS - 1)

            dve.wait_ge(cnt_s, 1)
            link(V.tensor_copy(cnt[:, :], route[:, 0:N_EXP]))
            link(V.tensor_scalar(cnti[:, :], cnt[:, :], float(P - 1), None, ALU.add))
            link(V.tensor_scalar(nti[:, :], cnti[:, :], 7, None, ALU.arith_shift_right))
            link(V.tensor_copy(ntf[:, :], nti[:, :]))
            link(V.tensor_tensor_scan(cin[:, :], ntf[:, :], zero_e[:, :], 0.0, ALU.add, ALU.add))
            link(V.tensor_tensor(cex[:, :], cin[:, :], ntf[:, :], ALU.subtract))
            link(V.tensor_tensor(ends[:, :], cnt[:, :], region[:, :], ALU.add))
            link(V.scalar_tensor_tensor(last_row[:, :], cex[:, :], float(P), ends[:, :], ALU.mult, ALU.add))
            link(V.tensor_scalar(ind2[:, :], cin[:, :], srow[:, :], None, ALU.is_gt))
            link(V.scalar_tensor_tensor(ind[:, :], cex[:, :], srow[:, :], ind2[:, :], ALU.is_le, ALU.mult))
            def pick(col, values):
                link(V.tensor_tensor_reduce(out=junk[:, :], in0=ind[:, :], in1=values, scale=1.0, scalar=0.0,
                                            op0=ALU.mult, op1=ALU.add, accum_out=tv[:, col:col + 1]))
            pick(0, iota_e[:, :])
            pick(2, last_row[:, :])
            pick(3, ind[:, :])
            c_ = lambda n: tv[:, n:n + 1]
            V.scalar_tensor_tensor(c_(1), c_(3), sback[:, :], c_(2), ALU.mult, ALU.add).then_inc(tv_s, 1)
            dve.wait_ge(tr_s, 1)
            V.tensor_copy(table[:, :], route[0:1, 0:2 * P]).then_inc(tab_s, 1)
            dve.wait_ge(tab_s, 1)
            dve.wait_ge(w1_in_s, 128)

            def pick_w1(it, c, e):
                dve.wait_ge(hp_s, it * RING + (c + 1))
                dve.wait_ge(h0_s, it * RING + (c + 1))
                dve.wait_ge(h1_s, it * RING + (c + 1))
                V.tensor_copy(w1s[:, c % 2, :], w1_sb[:, ds(e * W1C, W1C)]).then_inc(w1s_s, 1)

            def relu(it, c):
                dve.wait_ge(hp_s, it * RING + (c + 3))
                dve.wait_ge(yp_s, it * RING + (c + 1))
                dve.wait_ge(w1s_s, it * RING + (c + 1))
                V.tensor_scalar(ht[:, c % 2, 1, :], hp[c % 2][1][:, 0:P], w1s[:, c % 2, HID + 1:HID + 2], 0.0,
                                ALU.add, ALU.max).then_inc(h1_s, 1)

            expert_regs = entry_registers(dve, "w1_expert")
            first = load_entries(dve, expert_regs, 0, 3, N_EXP - 1)
            pick_w1(0, 0, first[0])
            pick_w1(0, 1, first[1])
            relu(0, 0)
            pick_w1(0, 2, first[2])

            def tiles_turn(it, n):
                picks = n if n == RING else n - 3
                experts = load_entries(dve, expert_regs, it * RING + 3, picks, N_EXP - 1)
                for c in range(n):
                    if n == RING or c + 1 < n:
                        relu(it + (c + 1) // RING, (c + 1) % RING)
                    if c < picks:
                        pick_w1(it + (c + 3) // RING, (c + 3) % RING, experts[c])

            expert_tiles(dve, tiles_turn)

            dve.wait_ge(hp_s, FTILES + 2)
            dve.wait_ge(w1s_s, FTILES)
            for c in range(2):
                last = V.memset(y_sb[c][96:P, TILES - 1, :], 0.0)
            last.then_inc(ypad_s, 1)
            for h, (t0, t1) in enumerate(CHUNKS):
                dve.wait_ge(y_in_s[h], 96 if t1 == TILES else 32)
                for c in range(2):
                    if c == 1:
                        dve.wait_ge(half_s, t1)
                    for t in range(t0, t1):
                        V.scalar_tensor_tensor(x_sb[:, t, :], y_sb[c][:, t, :], gates[:, t, c:c + 1], x_sb[:, t, :],
                                               ALU.mult, ALU.add).then_inc(half_s if c == 0 else out_s, 1)


def kernel(x, adj, L0_gnn_Wq, L0_gnn_Wk, L0_ffn_Wr, L0_ffn_br, L0_ffn_W1, L0_ffn_b1, L0_ffn_W2, L0_ffn_b2):
    import numpy as np
    import concourse.bacc as bacc
    from concourse import mybir as mb
    from concourse.bass_utils import run_bass_kernel_spmd

    x, adj, wq, wk, wr, br, w1, b1, w2, b2 = (np.asarray(a) for a in (
        x, adj, L0_gnn_Wq, L0_gnn_Wk, L0_ffn_Wr, L0_ffn_br, L0_ffn_W1, L0_ffn_b1, L0_ffn_W2, L0_ffn_b2))
    xp = np.zeros((NPAD, D), x.dtype)
    xp[:N_TOK] = x
    ap = np.zeros((NPAD, NPAD), adj.dtype)
    ap[:N_TOK, :N_TOK] = adj
    w1p = np.concatenate([w1.transpose(1, 0, 2), b1.reshape(N_EXP, 2, P).transpose(2, 0, 1)], axis=2)
    arrays = {
        "x_in": xp.reshape(TILES, P, D).transpose(1, 0, 2),
        "adj_in": ap,
        "wqk_in": np.concatenate([wq.T, wk.T], axis=1),
        "wr_in": wr,
        "br_in": np.broadcast_to(br[None, :], (P, N_EXP)),
        "w1_in": w1p.reshape(P, N_EXP * W1C),
        "w2_in": w2.reshape(N_EXP, 2, P, D).transpose(2, 0, 1, 3).reshape(P, N_EXP * HID),
        "b2_in": b2,
    }
    arrays = {n: np.ascontiguousarray(a) for n, a in arrays.items()}
    nc = bacc.Bacc("TRN2", target_bir_lowering=False, num_devices=1)
    args = [nc.dram_tensor(n, a.shape, mb.dt.from_np(a.dtype), kind="ExternalInput").ap() for n, a in arrays.items()]
    out = nc.dram_tensor("out", (P, TILES, D), mb.dt.float32, kind="ExternalOutput").ap()
    gnn_moe_program(nc, *args, out)
    r = run_bass_kernel_spmd(nc, [arrays], core_ids=[0])
    got = r.results[0]["out"]
    return got.transpose(1, 0, 2).reshape(NPAD, D)[:N_TOK]
```

```python
import concourse.bass as bass
from concourse import mybir
from contextlib import ExitStack

N_TOK, D, HID, N_EXP = 3327, 128, 256, 64
P = 128
TILES = -(-N_TOK // P)
NPAD = TILES * P
BLOCKS = TILES // 2
PAIRS = TILES // 2
CAP = NPAD + P
ROW = D + 2
FTILES = (2 * N_TOK + N_EXP * (P - 1)) // P
RING = 12
TURNS = FTILES // RING
REST = FTILES - TURNS * RING
XS_ROWS = N_EXP * CAP
YT_ROWS = 2 * NPAD
NOWHERE = 1 << 20
EPS = 1e-5
W1C = HID + 2
FXC = 2 * D + 1
LOOP_LINKS = 30
X_CHUNKS = ((0, 4), (4, 10), (10, 18), (18, TILES))
CHUNKS = ((0, 8), (8, 16), (16, 22), (22, TILES))
BIG = 3 * NPAD * 2


def gnn_moe_program(nc, x_in, adj_in, wqk_in, wr_in, br_in, w1_in, w2_in, b2_in, out):
    fp32, bf16, fp16 = mybir.dt.float32, mybir.dt.bfloat16, mybir.dt.float16
    i32, u32 = mybir.dt.int32, mybir.dt.uint32
    ALU, ACT, AX = mybir.AluOpType, mybir.ActivationFunctionType, mybir.AxisListType
    ds = bass.ds

    with ExitStack() as ctx:
        def sb(name, shape, dt):
            return ctx.enter_context(nc.sbuf_tensor(name, shape, dt))

        def sem(name):
            return ctx.enter_context(nc.semaphore(name))

        x_sb = sb("x_sb", [P, TILES, D], fp32)
        fx = sb("fx", [P, TILES, FXC], fp16)
        w1_sb = sb("w1_sb", [P, N_EXP * W1C], fp32)
        big = sb("big", [P, BIG], fp32)
        qk = big[:, 0:2 * NPAD].bitcast(fp16).rearrange("p (q n) -> p q n", q=4)
        raw = big[:, 2 * NPAD:4 * NPAD].bitcast(i32).rearrange("p (s n) -> p s n", s=2)
        mask = [big[:, (5 - b) * NPAD:(6 - b) * NPAD].bitcast(bf16).rearrange("p (s n) -> p s n", s=2)
                for b in range(2)]
        W2_AT = 5 * NPAD - N_EXP * HID
        w2_sb = big[:, W2_AT:5 * NPAD]
        f32_sb = w1_sb[:, 0:NPAD].rearrange("p (t d) -> p t d", d=D)
        s1 = w1_sb[:, NPAD:]
        ft = s1[:, 0:4 * P].rearrange("p (s u n) -> p s u n", s=2, u=2)
        sq = s1[:, 4 * P:12 * P].rearrange("p (s g h) -> p s g h", s=2, g=4)
        qn = s1[:, 12 * P:20 * P].rearrange("p (s g h) -> p s g h", s=2, g=4)
        hl = s1[:, 20 * P:28 * P].bitcast(fp16).rearrange("p (s g l n) -> p s g l n", s=2, g=4, l=2)
        y_sb = [w1_sb[:, c * NPAD:(c + 1) * NPAD].rearrange("p (t d) -> p t d", d=D) for c in range(2)]
        wqk = s1[:, 28 * P:30 * P]

        at = [30 * P]

        def setup_store(*shape):
            n = 1
            for d in shape:
                n *= d
            view = s1[:, at[0]:at[0] + n]
            at[0] += n
            if len(shape) == 2:
                view = view.rearrange("p (a b) -> p a b", a=shape[0])
            return view

        stats = setup_store(TILES, 6)
        moments = setup_store(TILES, 2)
        varep = setup_store(TILES)
        rstd = setup_store(TILES)
        shift = setup_store(PAIRS)
        ss = setup_store(PAIRS, 4)
        ssm = setup_store(PAIRS, 4)
        rn = setup_store(PAIRS, 4)
        p32 = sb("p32", [P, 3, 512], fp32)
        phi = sb("phi", [P, 3, 512], fp16)
        plo = sb("plo", [P, 3, 512], fp16)
        pay = sb("pay", [P, 2, 2, 2, ROW], fp32)
        c_all = sb("c_all", [P, 2, 2, N_EXP], bf16)
        id32 = sb("id32", [P, P], fp32)
        id16 = sb("id16", [P, P], fp16)
        idm = sb("idm", [P, P], bf16)
        tri = sb("tri", [P, P], bf16)
        ones = sb("ones", [P, P], bf16)
        wr = sb("wr", [P, N_EXP], fp32)
        br = sb("br", [P, N_EXP], fp32)
        b2 = sb("b2", [N_EXP, D], fp32)
        iota_e = sb("iota_e", [P, N_EXP], fp32)
        region = sb("region", [P, N_EXP], fp32)
        dest = sb("dest", [P, 2, TILES], i32)
        tok = sb("tok", [P, TILES], fp32)
        padx = sb("padx", [P, TILES], fp32)
        srow = sb("srow", [P, 1], fp32)
        sback = sb("sback", [P, 1], fp32)
        m_half = sb("m_half", [P, 4], fp32)
        zero_e = sb("zero_e", [P, N_EXP], fp32)
        padrow = sb("padrow", [P, ROW], fp32)
        guard = sb("guard", [P, 2], fp32)
        den = sb("den", [P, 2, 2], fp32)
        g_sb = sb("g_sb", [P, 3, 2, D], fp32)
        v_sb = sb("v_sb", [P, 2, D], fp32)
        st2 = sb("st2", [P, 2, 6], fp32)
        mv2 = sb("mv2", [P, 2, 2], fp32)
        ve2 = sb("ve2", [P, 2], fp32)
        r2 = sb("r2", [P, 2], fp32)
        zt = sb("zt", [P, 2, P], fp32)
        lg = sb("lg", [P, 2, N_EXP], fp32)
        top = sb("top", [P, 2, 8], fp32)
        tix = sb("tix", [P, 2, 8], u32)
        tixf = sb("tixf", [P, 2, 2], fp32)
        oh = sb("oh", [P, 2, 2, N_EXP], fp32)
        ohg = sb("ohg", [P, 2, 2, N_EXP], fp32)
        comb = sb("comb", [P, TILES, N_EXP], fp32)
        csum = sb("csum", [P, N_EXP], bf16)
        gap = sb("gap", [P, 2], fp32)
        eg = sb("eg", [P, 2], fp32)
        eg1 = sb("eg1", [P, 2], fp32)
        place = sb("place", [P, 2, N_EXP], fp32)
        pos = sb("pos", [P, 2, 2], fp32)
        posi = sb("posi", [P, 2, 2, 2], i32)
        gf = g_sb[:, :, :, :].rearrange("p a t d -> p (a t d)")
        ntf, cin, cex, ind, ind2, junk, ends, last_row = (gf[:, n * N_EXP:(n + 1) * N_EXP] for n in range(8))
        cnti, nti = (gf[:, n * N_EXP:(n + 1) * N_EXP].bitcast(i32) for n in (8, 9))
        tv = sb("tv", [P, 4], fp32)
        table = sb("table", [1, 2 * P], i32)
        combt = gf[0:N_EXP, 0:4 * P].rearrange("p (s u n) -> p s u n", s=2, u=2)
        p32f = p32[:, :, :].rearrange("p r n -> p (r n)")
        xt = p32f[:, 0:2 * P].rearrange("p (s n) -> p s n", s=2)
        w1s = p32f[:, 2 * P:2 * P + 2 * W1C].rearrange("p (s n) -> p s n", s=2)
        ht = p32f[:, 6 * P + 4:10 * P + 4].rearrange("p (s h n) -> p s h n", s=2, h=2)
        w2s = phi[:, :, :].rearrange("p r n -> p (r n)").bitcast(fp32).rearrange("p (s n) -> p s n", s=3)
        rings = big[:, 5 * NPAD:]
        xg = rings[:, 0:RING * ROW].rearrange("p (s n) -> p s n", s=RING)
        ys = rings[:, RING * ROW:RING * (ROW + D)].rearrange("p (s n) -> p s n", s=RING)

        def scratch(name, rows, cols):
            t = nc.dram_tensor(name, [rows, cols], fp32)
            return t.ap()

        xs = scratch("xs", XS_ROWS, ROW)
        yt = scratch("yt", YT_ROWS, D)

        score = [ctx.enter_context(nc.psum_tensor(f"score{i}", [P, 512], fp32)) for i in range(3)]
        acc = [ctx.enter_context(nc.psum_tensor(f"acc{i}", [P, 2, 512], fp32)) for i in range(2)]
        route = ctx.enter_context(nc.psum_tensor("route", [P, 512], fp32))
        ftp = [score[0], score[1]]
        qkp = [acc[0][:, 0, :], acc[0][:, 1, :]]
        qtp = [acc[1][:, c, :].bitcast(fp16).rearrange("p (u q n) -> p u q n", u=2, q=4) for c in range(2)]
        xtp = [score[0], score[1]]
        hp = [[acc[0][:, 0, :], acc[0][:, 1, :]], [acc[1][:, 0, :], acc[1][:, 1, :]]]
        yp = [score[2], route]
        cbp = [score[0], score[1]]
        b2p = [acc[c // 2][:, c % 2, :] for c in range(4)]

        x_in_s = [sem(f"x_loaded{c}") for c in range(len(X_CHUNKS))]
        wqk_in_s = sem("wq_wk_loaded")
        w_in_s = sem("weights_loaded")
        adj_in_s = [sem(f"adj_loaded{s}") for s in range(2)]
        w1_in_s = sem("w1_loaded")
        w2_in_s = sem("w2_loaded")
        id_s = sem("identity_made")
        const_s = sem("constants_made")
        chain_s = sem("dve_step")
        pchain_s = sem("pool_step")
        pstep_s = sem("pool_route_step")
        bn_s = sem("x_row_stats")
        hi_s = sem("high_parts_made")
        half_s = sem("first_choice_added")
        v_s = sem("low_share_added")
        st2_s = sem("x1_row_stats")
        tix_s = sem("choices_found")
        lgb_s = sem("logits_biased")
        ypad_s = sem("y_padding_made")
        stats_s = sem("stats_made")
        rstd_s = sem("rstd_made")
        shift_s = sem("shifts_made")
        f_s = sem("f_of_even_tiles_made")
        fodd_s = sem("f_of_odd_tiles_made")
        fhi_s = sem("f_high_made")
        fx_s = sem("fx_made")
        ftp_s = sem("f_transposed")
        ft_s = sem("f_transposed_copied")
        qk_s = sem("qk_projected")
        sq_s = sem("squares_made")
        qn_s = sem("qk_normalised")
        ss_s = sem("squares_summed")
        rn_s = sem("row_norms_made")
        hl_s = sem("qk_split")
        qt_s = sem("qk_transposed")
        qtc_s = sem("qk_transposed_copied")
        mask_s = sem("mask_made")
        mask0_s = sem("first_mask_half_made")
        score_s = sem("scores_made")
        exp_s = sem("exponentials_made")
        lo_s = sem("low_parts_made")
        pv_s = sem("pair_accumulated")
        den_s = sem("guards_made")
        u_s = sem("residual_made")
        accread_s = sem("accumulators_read")
        mv_s = sem("moments_made")
        r2_s = sem("rstd2_made")
        z_s = sem("z_made")
        pay_s = sem("payload_made")
        ztp_s = sem("z_transposed")
        zt_s = sem("z_transposed_copied")
        lg_s = sem("logits_made")
        cho_s = sem("choices_made")
        eg_s = sem("gate_exponentials_made")
        cmb_s = sem("combine_made")
        rank_s = sem("ranks_made")
        pos_s = sem("positions_made")
        cbt_s = sem("combine_transposed")
        cbc_s = sem("combine_transposed_copied")
        b2_s = sem("b2_share_made")
        b2a_s = sem("b2_share_added")
        scat_s = [sem(f"rows_scattered{c}") for c in range(2)]
        cnt_s = sem("counts_made")
        tv_s = sem("table_columns_made")
        tr_s = sem("table_rows_made")
        tab_s = sem("table_made")
        padw_s = sem("padding_written")
        xg_s = [sem(f"tile_loaded{c}") for c in range(RING)]
        xtp_s = sem("tile_transposed")
        xt_s = sem("tile_transposed_copied")
        w1s_s = sem("w1_picked")
        w2s_s = sem("w2_picked")
        hp_s = sem("hidden_made")
        h0_s = sem("hidden0_activated")
        h1_s = sem("hidden1_activated")
        yp_s = sem("results_made")
        ys_s = [sem(f"results_copied{c}") for c in range(RING)]
        ysc_s = [sem(f"results_scattered{c}") for c in range(RING)]
        y_in_s = [[sem(f"y{c}_loaded{h}") for c in range(2)] for h in range(len(CHUNKS))]
        out_s = sem("combined")
        st_s = sem("stored")

        def slot(b_odd, k):
            return (k + b_odd) % 3

        def since(b_odd, k):
            n = 1
            while True:
                q = k - n
                odd = b_odd if q >= 0 else 1 - b_odd
                if slot(odd, q % PAIRS) == slot(b_odd, k):
                    return n
                n += 1

        def at_once(eng):
            eng.wait_ge(const_s, 1)

        def expert_tiles(eng, turn):
            turn(0, RING)
            with eng.Fori(1, TURNS) as it:
                turn(it, RING)
            turn(TURNS, REST)

        def wait_scattered(eng, it, c):
            if not isinstance(it, int) or it > 0:
                eng.wait_ge(ysc_s[c], it * 16)

        def setup_rounds(stages, start=-4, stop=PAIRS + 2):
            for i in range(start, stop):
                for lag, stage in stages:
                    if 0 <= i - lag < PAIRS:
                        stage(i - lag)

        def entry_registers(eng, name):
            return [eng.alloc_register(f"{name}{c}") for c in range(RING + 1)]

        def load_entries(eng, regs, col, n, top):
            eng.load(regs[:n], table[0:1, ds(col, n)])
            return [eng.snap(r, min_val=0, max_val=top) for r in regs[:n]]

        block = ctx.enter_context(nc.Block())

        @block.sync
        def _(sp):
            for c, (t0, t1) in enumerate(X_CHUNKS):
                sp.dma_start(x_sb[:, t0:t1, :], x_in[:, t0:t1, :]).then_inc(x_in_s[c], 16)

            def load_adj(t, s):
                sp.dma_start(raw[:, s, :], adj_in[ds(t * P, P), :]).then_inc(adj_in_s[s], 16)

            for s in range(2):
                load_adj(s, s)
            sp.wait_ge(const_s, 1)
            sp.dma_start(xs.rearrange("(e r) d -> r e d", r=CAP)[0:P],
                         padrow[:, None, :].to_broadcast([P, N_EXP, ROW]))\
              .then_inc(padw_s, 16)
            W1P = N_EXP * W1C // 8
            with sp.Fori(1, 9) as b:
                for s in range(2):
                    sp.wait_ge(mask_s, b * 2 + (s - 1))
                    load_adj(b * 2 + s, s)
                sp.wait_ge(qtc_s, PAIRS)
                sp.wait_ge(fx_s, PAIRS)
                sp.dma_start(w1_sb[:, ds((b - 1) * W1P, W1P)], w1_in[:, ds((b - 1) * W1P, W1P)])\
                  .then_inc(w1_in_s, 16)
            with sp.Fori(9, BLOCKS) as b:
                for s in range(2):
                    sp.wait_ge(mask_s, b * 2 + (s - 1))
                    load_adj(b * 2 + s, s)
            def load_w2(a, b):
                sp.dma_start(big[:, a:b], w2_in[:, a - W2_AT:b - W2_AT]).then_inc(w2_in_s, 16)

            K0, K1 = NPAD, 3 * NPAD // 2
            last = (NPAD - 2 * P) // 2
            sp.wait_ge(mask_s, TILES)
            load_w2(2 * NPAD, 4 * NPAD)
            sp.wait_ge(score_s, (BLOCKS - 1) * PAIRS)
            load_w2(4 * NPAD, 5 * NPAD)
            load_w2(K0, K0 + last)
            load_w2(K1, K1 + last)
            sp.wait_ge(score_s, BLOCKS * PAIRS)
            load_w2(W2_AT, K0)
            load_w2(K0 + last, K1)
            load_w2(K1 + last, 2 * NPAD)
            sp.wait_ge(tab_s, 1)
            for c in range(2):
                sp.wait_ge(scat_s[c], 64 * (BLOCKS // 2 + (1 - c)))
            row_regs = entry_registers(sp, "row")

            def load_turn(it, n):
                for c0 in range(0, n, 4):
                    some = min(4, n - c0)
                    rows = load_entries(sp, row_regs[c0:], it * RING + (P + c0), some, XS_ROWS - P)
                    for c in range(c0, c0 + some):
                        wait_scattered(sp, it, c)
                        sp.dma_start(xg[:, c, :], xs[ds(rows[c - c0], P), :]).then_inc(xg_s[c], 16)

            expert_tiles(sp, load_turn)
            for c in range(RING):
                sp.wait_ge(ysc_s[c], (TURNS + (c < REST)) * 16)
            sp.wait_ge(ypad_s, 1)
            for h, (t0, t1) in enumerate(CHUNKS):
                whole = min(t1, TILES - 1)
                for c in range(2):
                    src = yt[c * NPAD:(c + 1) * NPAD, :].rearrange("(t p) d -> p t d", p=P)
                    sp.dma_start(y_sb[c][:, t0:whole, :], src[:, t0:whole, :]).then_inc(y_in_s[h][c], 16)
                    if t1 == TILES:
                        sp.dma_start(y_sb[c][0:112, t1 - 1, :], src[0:112, t1 - 1, :]).then_inc(y_in_s[h][c], 16)
                        sp.dma_start(y_sb[c][112:127, t1 - 1, :], src[112:127, t1 - 1, :]).then_inc(y_in_s[h][c], 16)
            for h, (t0, t1) in enumerate(CHUNKS):
                sp.wait_ge(out_s, h + 1)
                sp.dma_start(out[:, t0:t1, :], x_sb[:, t0:t1, :]).then_inc(st_s, 16)
            sp.wait_ge(st_s, 16 * len(CHUNKS))

        @block.gpsimd
        def _(pool):
            count = [0]

            def link(ins):
                count[0] += 1
                ins.then_inc(pchain_s, 1)
                pool.wait_ge(pchain_s, count[0])

            link(pool.memset(m_half[:, :], -0.5))

            def diagonal(m, value):
                link(pool.memset(m[:, :], 0.0))
                return pool.affine_select(out=m[:, :], in_=m[:, :], compare_op=ALU.not_equal, fill=value,
                                          base=0, pattern=[[-1, P]], channel_multiplier=1)

            diagonal(id32, 1.0).then_inc(id_s, 1)
            link(diagonal(id16, 1.0))
            link(diagonal(idm, 32768.0))
            link(pool.memset(ones[:, :], 1.0))
            link(pool.affine_select(out=tri[:, :], in_=ones[:, :], compare_op=ALU.is_gt, fill=0.0,
                                    base=0, pattern=[[1, P]], channel_multiplier=-1))

            def row_scale(m):
                pool.wait_ge(stats_s, m + 1)
                two = slice(2 * m, 2 * m + 2)
                link(pool.tensor_scalar(varep[:, two], moments[:, two, 1], EPS, None, ALU.add))
                pool.tensor_tensor(rstd[:, two], varep[:, two], m_half[:, 0:2], ALU.pow).then_inc(rstd_s, 1)

            setup_rounds(((-4, row_scale),), stop=-2)
            link(pool.memset(csum[:, :], 0.0))
            link(pool.memset(zero_e[:, :], 0.0))
            link(pool.memset(padrow[:, :], 0.0))
            link(pool.iota(iota_e[:, :], [[1, N_EXP]], base=0, channel_multiplier=0,
                           allow_small_or_imprecise_dtypes=True))
            link(pool.iota(dest[:, :, :], [[NPAD, 2], [P, TILES]], base=0, channel_multiplier=1))
            link(pool.iota(tok[:, :], [[P, TILES]], base=0, channel_multiplier=1,
                           allow_small_or_imprecise_dtypes=True))
            link(pool.iota(srow[:, :], [[0, 1]], base=0, channel_multiplier=1,
                           allow_small_or_imprecise_dtypes=True))
            link(pool.iota(padrow[:, D:D + 1].bitcast(i32), [[0, 1]], base=NOWHERE, channel_multiplier=0))
            link(pool.tensor_scalar(region[:, :], iota_e[:, :], float(CAP), float(P), ALU.mult, ALU.add))
            link(pool.tensor_scalar(padx[:, :], tok[:, :], float(N_TOK), float(NOWHERE), ALU.is_ge, ALU.mult))
            pool.tensor_scalar(sback[:, :], srow[:, :], -float(P), -float(P), ALU.mult, ALU.add)\
                .then_inc(const_s, 1)

            def norm_scale(m):
                pool.wait_ge(ss_s, m + 1)
                link(pool.tensor_scalar(ssm[:, m, :], ss[:, m, :], 1e-8, None, ALU.max))
                pool.tensor_tensor(rn[:, m, :], ssm[:, m, :], m_half[:, :], ALU.pow).then_inc(rn_s, 1)

            def f_low(m):
                pool.wait_ge(fhi_s, m + 1)
                two = slice(2 * m, 2 * m + 2)
                pool.tensor_tensor(fx[:, two, 0:D], f32_sb[:, two, :], fx[:, two, D:2 * D], ALU.subtract)\
                    .then_inc(fx_s, 1)

            setup_rounds(((0, norm_scale), (-4, row_scale), (-1, f_low)), start=-2)
            pool.wait_ge(fx_s, PAIRS)

            def residual(e, hurry):
                fx2 = fx[:, ds(e * 2, 2), :]
                pool.tensor_tensor(g_sb[:, 0], fx2[:, :, 0:D], fx2[:, :, D:2 * D], ALU.add)\
                    .then_inc(pstep_s, 2 if hurry else 1)
                if hurry:
                    return
                pool.wait_ge(den_s, e + 1)
                pool.wait_ge(pstep_s, e * 4 + 1)
                pool.tensor_tensor(g_sb[:, 1], g_sb[:, 0], guard[:, :, None].to_broadcast([P, 2, D]), ALU.mult)\
                    .then_inc(pstep_s, 1)
                pool.wait_ge(pstep_s, e * 4 + 2)
                pool.tensor_tensor(g_sb[:, 2], g_sb[:, 1], x_sb[:, ds(e * 2, 2), :], ALU.add).then_inc(u_s, 1)

            def second_norm(e, odd):
                at_once(pool)
                pool.wait_ge(mv_s, e + 1)
                pool.tensor_scalar(ve2[:, :], mv2[:, :, 1], EPS, None, ALU.add).then_inc(pstep_s, 1)
                pool.wait_ge(pstep_s, e * 4 + 3)
                pool.tensor_tensor(r2[:, :], ve2[:, :], m_half[:, 0:2], ALU.pow).then_inc(r2_s, 1)

            def payload(e, odd):
                pool.tensor_copy(pay[:, odd, :, :, D:D + 1].bitcast(i32),
                                 dest[:, :, ds(e * 2, 2)].rearrange("p c t -> p t c")[:, :, :, None])\
                    .then_inc(pstep_s, 1)
                at_once(pool)
                pool.wait_ge(z_s, e + 1)
                pool.tensor_copy(pay[:, odd, :, 1, 0:D], pay[:, odd, :, 0, 0:D]).then_inc(pay_s, 1)

            def scatters(e, odd):
                at_once(pool)
                pool.wait_ge(pos_s, e + 1)
                pool.wait_ge(pay_s, e + 1)
                for t in range(2):
                    for c in range(2):
                        pool.indirect_dma_start(
                            out=xs[:, :], out_offset=bass.IndirectOffsetOnAxis(ap=posi[:, odd, t, c:c + 1], axis=0),
                            in_=pay[:, odd, t, c, :], in_offset=None,
                            bounds_check=XS_ROWS - 1, oob_is_err=False).then_inc(scat_s[odd], 16)

            pool.wait_ge(const_s, 1)
            pool.wait_ge(padw_s, 16)

            def body(e, odd, again=True, behind=True, hurry=False):
                residual(e, hurry)
                if behind and not hurry:
                    scatters(e - 1, 1 - odd)
                second_norm(e, odd)
                at_once(pool)
                if again:
                    pool.wait_ge(scat_s[odd], (e - odd) * 32)
                payload(e, odd)
                if hurry:
                    scatters(e - 1, 1 - odd)

            body(0, 0, again=False, behind=False)
            body(1, 1, again=False)
            with pool.Fori(1, (BLOCKS - 1) // 2) as it:
                for u in range(2):
                    body(it * 2 + u, u)
            body(BLOCKS - 1, 0, hurry=True)
            scatters(BLOCKS - 1, 0)

            def send_turn(nth, n):
                for c in range(n):
                    at_once(pool)
                    pool.wait_ge(ys_s[c], nth)
                    pool.indirect_dma_start(
                        out=yt[:, :], out_offset=bass.IndirectOffsetOnAxis(ap=xg[:, c, D:D + 1].bitcast(i32), axis=0),
                        in_=ys[:, c, :], in_offset=None, bounds_check=YT_ROWS - 1, oob_is_err=False)\
                        .then_inc(ysc_s[c], 16)

            with pool.Fori(1, TURNS + 1) as nth:
                send_turn(nth, RING)
            send_turn(TURNS + 1, REST)

        @block.tensor
        def _(pe):
            mm = nc.tensor.matmul
            pe.wait_ge(id_s, 1)

            def stay_awake(bank, lhs, rhs, n):
                for _ in range(n):
                    mm(bank, lhs, rhs, start=True, stop=True)

            stay_awake(score[2][:, 0:P], id32[:, :], id32[:, :], 10)

            def transpose_f(m):
                pe.wait_ge(f_s, m + 1)
                pe.wait_ge(fodd_s, m + 1)
                if m >= 2:
                    pe.wait_ge(ft_s, m - 1)
                for u in range(2):
                    last = nc.tensor.transpose(ftp[m % 2][:, P * u:P * u + P], f32_sb[:, 2 * m + u, :], id32[:, :])
                last.then_inc(ftp_s, 1)

            def project(m):
                if m == 0:
                    pe.wait_ge(wqk_in_s, 16)
                pe.wait_ge(ft_s, m + 1)
                if m >= 2:
                    pe.wait_ge(qn_s, m - 1)
                for u in range(2):
                    last = mm(qkp[m % 2][:, 256 * u:256 * u + 256], ft[:, m % 2, u, :], wqk[:, :],
                              start=True, stop=True)
                last.then_inc(qk_s, 1)

            def transpose_qk(m):
                if m == 0:
                    pe.wait_ge(const_s, 1)
                    pe.wait_ge(w_in_s, 48)
                pe.wait_ge(hl_s, m + 1)
                if m >= 2:
                    pe.wait_ge(qtc_s, m - 1)
                for u in range(2):
                    for q in range(4):
                        last = nc.tensor.transpose(qtp[m % 2][:, u, q, :], hl[:, m % 2, 2 * u + q // 2, q % 2, :],
                                                   id16[:, :])
                last.then_inc(qt_s, 1)

            def scores(b, odd, k):
                p = b * PAIRS + k
                r = slot(odd, k)
                if isinstance(b, int) and b == 0:
                    pe.wait_ge(qtc_s, k + 1)
                    if k == 0:
                        pe.wait_ge(ft_s, PAIRS)
                        pe.wait_ge(mask0_s, 2)
                    if k == PAIRS // 2:
                        pe.wait_ge(mask_s, 2)
                elif k == 0:
                    pe.wait_ge(mask_s, b * 2 + 2)
                pe.wait_ge(exp_s, p - since(odd, k) + 4)
                for j in range(2):
                    o = score[r][:, 256 * j:256 * j + 256]
                    cols = slice((2 * k + j) * P, (2 * k + j + 1) * P)
                    for i in range(2):
                        mm(o[:, P * i:P * i + P], mask[odd][:, i, cols], idm[:, :],
                           start=(j == 0 and i == 0), stop=False, skip_group_check=True)
                    for n, (a, c) in enumerate(((0, 2), (0, 3), (1, 2))):
                        last = mm(o, qk[:, a, cols], qk[:, c, ds(b * 256, 256)],
                                  start=False, stop=(n == 2 and j == 1), skip_group_check=True)
                last.then_inc(score_s, 1)

            def accumulate(b, odd, k):
                p = b * PAIRS + k
                r = slot(odd, k)
                if k == 0 and not (isinstance(b, int) and b < 2):
                    pe.wait_ge(accread_s, b - 1)
                if isinstance(b, int) and b == 0:
                    pe.wait_ge(fx_s, k + 1)
                    if k == 0:
                        pe.wait_ge(qn_s, PAIRS)
                pe.wait_ge(lo_s, p + 1)
                for j in range(2):
                    t = 2 * k + j
                    for i in range(2):
                        w = slice(256 * j + P * i, 256 * j + P * i + P)
                        mm(acc[odd][:, i, 0:FXC], phi[:, r, w], fx[:, t, :],
                           start=(t == 0), stop=False, skip_group_check=True)
                        last = mm(acc[odd][:, i, D:FXC], plo[:, r, w], fx[:, t, D:FXC],
                                  start=False, stop=(t == TILES - 1), skip_group_check=True)
                last.then_inc(pv_s, 1)

            def route_zt(e, odd):
                pe.wait_ge(z_s, e + 1)
                if not (isinstance(e, int) and e == 0):
                    pe.wait_ge(pos_s, e)
                for t in range(2):
                    last = nc.tensor.transpose(route[:, P * t:P * t + P], pay[:, odd, t, 0, 0:D], id32[:, :])
                last.then_inc(ztp_s, 1)

            def route_logits(e):
                pe.wait_ge(zt_s, e + 1)
                for t in range(2):
                    last = mm(route[:, 256 + 64 * t:320 + 64 * t], zt[:, t, :], wr[:, :], start=True, stop=True)
                last.then_inc(lg_s, 1)

            def route_ranks(e, odd):
                pe.wait_ge(cho_s, e + 1)
                for t in range(2):
                    o = route[:, 384 + 64 * t:448 + 64 * t]
                    mm(o, tri[:, :], c_all[:, odd, t, :], start=True, stop=False)
                    last = mm(o, ones[:, :], csum[:, :], start=False, stop=(t == 0))
                    if t == 1:
                        last = mm(o, ones[:, :], c_all[:, odd, 0, :], start=False, stop=True)
                last.then_inc(rank_s, 1)

            def route_step(e, odd, k):
                if k == 7:
                    route_zt(e, odd)
                if k == 8:
                    route_logits(e)
                if k == 11:
                    route_ranks(e, odd)

            def first_scores(m):
                if m == PAIRS - 1:
                    scores(0, 0, 0)

            setup_rounds(((-1, transpose_f), (2, first_scores), (2, transpose_qk), (-1, project)))
            scores(0, 0, 1)

            def body(b, odd, routed=True, ahead=True):
                for k in range(PAIRS):
                    if routed:
                        route_step(b - 1, 1 - odd, k)
                    if k + 2 < PAIRS:
                        scores(b, odd, k + 2)
                    elif ahead:
                        scores(b + 1, 1 - odd, k + 2 - PAIRS)
                    accumulate(b, odd, k)

            body(0, 0, routed=False)
            body(1, 1)
            with pe.Fori(1, (BLOCKS - 1) // 2) as it:
                for u in range(2):
                    body(it * 2 + u, u)
            body(BLOCKS - 1, 0, ahead=False)
            pe.wait_ge(accread_s, BLOCKS - 1)
            idle = acc[1][:, 0, 0:2 * P], id16[:, :], fx[:, 0, 0:2 * P]
            stay_awake(*idle, 40)
            for k in range(PAIRS):
                route_step(BLOCKS - 1, 0, k)
                if k == 8:
                    stay_awake(*idle, 18)
            for n, c in enumerate((csum[:, :], c_all[:, 0, 0, :], c_all[:, 0, 1, :])):
                last = mm(score[0][:, 0:N_EXP], ones[:, :], c, start=(n == 0), stop=(n == 2))
            last.then_inc(cnt_s, 1)
            stay_awake(*idle, 30)
            pe.wait_ge(tv_s, 1)
            for c in range(2):
                last = mm(score[1][0:1, P * c:P * c + P], tv[:, c:c + 1], id32[:, :], start=True, stop=True)
            last.then_inc(tr_s, 1)
            stay_awake(*idle, 36)

            def transpose_tile(it, c):
                pe.wait_ge(xg_s[c], it * 16 + 16)
                pe.wait_ge(xt_s, it * RING + (c + 1))
                nc.tensor.transpose(xtp[c % 2][:, 0:P], xg[:, c, 0:D], id32[:, :]).then_inc(xtp_s, 1)

            def hidden(it, c):
                pe.wait_ge(xt_s, it * RING + (c + 3))
                pe.wait_ge(w1s_s, it * RING + (c + 1))
                pe.wait_ge(h0_s, it * RING + (c + 1))
                pe.wait_ge(h1_s, it * RING + (c + 1))
                for h in range(2):
                    last = mm(hp[c % 2][h][:, 0:P], w1s[:, c % 2, P * h:P * h + P], xt[:, c % 2, :],
                              start=True, stop=True)
                last.then_inc(hp_s, 1)

            def results(it, c):
                pe.wait_ge(w2s_s, it * RING + (c + 1))
                pe.wait_ge(h0_s, it * RING + (c + 3))
                pe.wait_ge(h1_s, it * RING + (c + 3))
                if c >= 2:
                    pe.wait_ge(ys_s[c - 2], it + 1)
                elif not isinstance(it, int) or it > 0:
                    pe.wait_ge(ys_s[c - 2 + RING], it)
                for h in range(2):
                    last = mm(yp[c % 2][:, 0:D], ht[:, c % 2, h, :], w2s[:, c % 3, P * h:P * h + P],
                              start=(h == 0), stop=(h == 1))
                last.then_inc(yp_s, 1)

            transpose_tile(0, 0)
            transpose_tile(0, 1)
            hidden(0, 0)

            def tiles_turn(it, n):
                for c in range(n):
                    for ahead, stage in ((2, transpose_tile), (1, hidden)):
                        if n == RING or c + ahead < n:
                            stage(it + (c + ahead) // RING, (c + ahead) % RING)
                    results(it, c)

            expert_tiles(pe, tiles_turn)

            for done in (xt_s, h0_s, h1_s):
                pe.wait_ge(done, FTILES + 2)
            pe.wait_ge(cmb_s, BLOCKS)

            def transpose_gates(m):
                if m >= 2:
                    pe.wait_ge(cbc_s, m - 1)
                for t in range(2):
                    last = nc.tensor.transpose(cbp[m % 2][0:N_EXP, P * t:P * t + P], comb[:, 2 * m + t, :],
                                               id32[:, :])
                last.then_inc(cbt_s, 1)

            transpose_gates(0)
            for m in range(BLOCKS):
                if m + 1 < BLOCKS:
                    transpose_gates(m + 1)
                pe.wait_ge(cbc_s, m + 1)
                if m >= 4:
                    pe.wait_ge(b2a_s, m - 3)
                for t in range(2):
                    last = mm(b2p[m % 4][:, P * t:P * t + P], combt[:, m % 2, t, :], b2[:, :], start=True, stop=True)
                last.then_inc(b2_s, 1)

        @block.scalar
        def _(act):
            A = nc.scalar.activation
            act.dma_start(wqk[:, :], wqk_in[:, :]).then_inc(wqk_in_s, 16)
            act.dma_start(wr[:, :], wr_in[:, :]).then_inc(w_in_s, 16)
            act.dma_start(br[:, :], br_in[:, :]).then_inc(w_in_s, 16)
            act.dma_start(b2[:, :], b2_in[:, :]).then_inc(w_in_s, 16)
            act.sem_inc(exp_s, 3)
            act.sem_inc(xt_s, 2)
            act.sem_inc(h0_s, 2)

            def squares(m):
                act.wait_ge(qk_s, m + 1)
                if m >= 2:
                    act.wait_ge(ss_s, m - 1)
                A(sq[:, m % 2, :, :], qkp[m % 2].rearrange("p (g h) -> p g h", g=4), ACT.Square).then_inc(sq_s, 1)

            def qk_high(m):
                act.wait_ge(qn_s, m + 1)
                if m >= 2:
                    act.wait_ge(qt_s, m - 1)
                A(hl[:, m % 2, :, 0, :], qn[:, m % 2, :, :], ACT.Copy).then_inc(hi_s, 1)

            def copy_ft(m):
                act.wait_ge(ftp_s, m + 1)
                if m >= 2:
                    act.wait_ge(qk_s, m - 1)
                A(ft[:, m % 2, :, :], ftp[m % 2][:, 0:2 * P].rearrange("p (u n) -> p u n", u=2), ACT.Copy)\
                    .then_inc(ft_s, 1)

            def f_high(m):
                act.wait_ge(f_s, m + 1)
                act.wait_ge(fodd_s, m + 1)
                A(fx[:, 2 * m:2 * m + 2, D:2 * D], f32_sb[:, 2 * m:2 * m + 2, :], ACT.Copy).then_inc(fhi_s, 1)

            def copy_qk(m):
                act.wait_ge(qt_s, m + 1)
                A(qk[:, :, 256 * m:256 * m + 256].rearrange("p q (u n) -> p u q n", u=2), qtp[m % 2], ACT.Copy)\
                    .then_inc(qtc_s, 1)

            act.wait_ge(id_s, 1)
            A(eg[:, :], id32[:, 0:2], ACT.Exp)

            def normalise_odd(m):
                act.wait_ge(shift_s, m + 1)
                A(f32_sb[:, 2 * m + 1, :], x_sb[:, 2 * m + 1, :], ACT.Identity, scale=rstd[:, 2 * m + 1:2 * m + 2],
                  bias=shift[:, m:m + 1]).then_inc(fodd_s, 1)


            def exps(b, odd, k):
                p = b * PAIRS + k
                r = slot(odd, k)
                act.wait_ge(score_s, p + 1)
                act.wait_ge(pv_s, p - since(odd, k) + 4)
                A(p32[:, r, :], score[r][:, :], ACT.Exp)
                A(phi[:, r, :], score[r][:, :], ACT.Exp).then_inc(exp_s, 1)

            def route_step(e, k):
                if k == 8:
                    act.wait_ge(ztp_s, e + 1)
                    A(zt[:, :, :], route[:, 0:256].rearrange("p (t n) -> p t n", t=2), ACT.Copy).then_inc(zt_s, 1)
                if k == 11:
                    act.wait_ge(tix_s, e + 1)
                    A(eg[:, :], gap[:, :], ACT.Exp).then_inc(eg_s, 1)

            def body(b, odd, routed=True, first=0):
                for k in range(first, PAIRS):
                    exps(b, odd, k)
                    if routed:
                        route_step(b - 1, k)

            def first_exps(m):
                if m == PAIRS - 1:
                    exps(0, 0, 0)

            setup_rounds(((-1, normalise_odd), (0, squares), (1, qk_high), (-1, copy_ft), (-1, f_high),
                          (2, first_exps), (2, copy_qk)))
            body(0, 0, routed=False, first=1)
            body(1, 1)
            with act.Fori(1, (BLOCKS - 1) // 2) as it:
                for u in range(2):
                    body(it * 2 + u, u)
            body(BLOCKS - 1, 0)
            for k in range(PAIRS):
                route_step(BLOCKS - 1, k)

            def tile_in(it, c):
                act.wait_ge(xtp_s, it * RING + (c + 1))
                act.wait_ge(hp_s, it * RING + (c + 1))
                A(xt[:, c % 2, :], xtp[c % 2][:, 0:P], ACT.Copy).then_inc(xt_s, 1)

            def relu(it, c):
                act.wait_ge(hp_s, it * RING + (c + 3))
                act.wait_ge(yp_s, it * RING + (c + 1))
                A(ht[:, c % 2, 0, :], hp[c % 2][0][:, 0:P], ACT.Relu, bias=w1s[:, c % 2, HID:HID + 1])\
                    .then_inc(h0_s, 1)

            def result(it, c):
                act.wait_ge(yp_s, it * RING + (c + 3))
                wait_scattered(act, it, c)
                A(ys[:, c, :], yp[c % 2][:, 0:D], ACT.Copy, scale=xg[:, c, D + 1:ROW]).then_inc(ys_s[c], 1)

            tile_in(0, 0)
            tile_in(0, 1)
            relu(0, 0)

            def tiles_turn(it, n):
                for c in range(n):
                    for ahead, stage in ((2, tile_in), (1, relu)):
                        if n == RING or c + ahead < n:
                            stage(it + (c + ahead) // RING, (c + ahead) % RING)
                    result(it, c)

            expert_tiles(act, tiles_turn)

            for m in range(BLOCKS):
                act.wait_ge(cbt_s, m + 1)
                if m >= 2:
                    act.wait_ge(b2_s, m - 1)
                A(combt[:, m % 2, :, :], cbp[m % 2][0:N_EXP, 0:2 * P].rearrange("p (t n) -> p t n", t=2), ACT.Copy)\
                    .then_inc(cbc_s, 1)

        @block.vector
        def _(dve):
            V = nc.vector
            count = [0, 0]

            def link(ins):
                count[0] += 1
                ins.then_inc(chain_s, 1)
                dve.wait_ge(chain_s, count[1] + count[0])

            dve.sem_inc(pv_s, 3)
            for credit in (h1_s, hp_s, yp_s):
                dve.sem_inc(credit, 2)
            V.memset(fx[:, :, 2 * D:FXC], 1.0)

            def convert(t, odd, s, part, parts):
                w = NPAD // parts
                cols = slice(part * w, (part + 1) * w)
                if part == 0:
                    dve.wait_ge(adj_in_s[s], (t - s) * 8 + 16)
                return V.tensor_scalar(mask[odd][:, s, cols], raw[:, s, cols], 0.0, 1.0, ALU.is_gt, ALU.subtract)

            def row_moments(m):
                for c, (t0, _) in enumerate(X_CHUNKS):
                    if t0 == 2 * m:
                        dve.wait_ge(x_in_s[c], 16)
                for t in (2 * m, 2 * m + 1):
                    V.bn_stats(stats[:, t, :], x_sb[:, t, :]).then_inc(bn_s, 1)
                dve.wait_ge(bn_s, 2 * m + 2)
                for t in (2 * m, 2 * m + 1):
                    last = V.bn_aggr(moments[:, t, :], stats[:, t, :])
                last.then_inc(stats_s, 1)

            def row_shift(m):
                dve.wait_ge(rstd_s, m + 1)
                t = 2 * m + 1
                V.scalar_tensor_tensor(shift[:, m:m + 1], moments[:, t, 0:1], -1.0, rstd[:, t:t + 1],
                                       ALU.mult, ALU.mult).then_inc(shift_s, 1)

            def normalise_even(m):
                dve.wait_ge(rstd_s, m + 1)
                t = 2 * m
                V.tensor_scalar(f32_sb[:, t, :], x_sb[:, t, :], moments[:, t, 0:1], rstd[:, t:t + 1],
                                ALU.subtract, ALU.mult).then_inc(f_s, 1)

            def sum_squares(m):
                dve.wait_ge(sq_s, m + 1)
                V.tensor_reduce(ss[:, m, :], sq[:, m % 2, :, :], AX.X, ALU.add).then_inc(ss_s, 1)

            def normalise_qk(m):
                dve.wait_ge(rn_s, m + 1)
                if m >= 2:
                    dve.wait_ge(hl_s, m - 1)
                V.tensor_tensor(qn[:, m % 2, :, :], qkp[m % 2].rearrange("p (g h) -> p g h", g=4),
                                rn[:, m, :, None].to_broadcast([P, 4, D]), ALU.mult).then_inc(qn_s, 1)

            def qk_low(m):
                dve.wait_ge(hi_s, m + 1)
                V.tensor_tensor(hl[:, m % 2, :, 1, :], qn[:, m % 2, :, :], hl[:, m % 2, :, 0, :], ALU.subtract)\
                 .then_inc(hl_s, 1)

            def first_mask(m):
                n = m - (PAIRS - 4)
                if n >= 0:
                    c = convert(n % 2, 0, n % 2, n // 2, 2)
                    c.then_inc(mask0_s if n < 2 else mask_s, 1)

            setup_rounds(((-2, row_shift), (-1, normalise_even), (0, sum_squares), (-4, row_moments), (1, qk_low),
                          (0, normalise_qk), (1, first_mask)))

            dve.wait_ge(const_s, 1)
            dve.wait_ge(w_in_s, 48)

            def low(b, odd, k):
                p = b * PAIRS + k
                r = slot(odd, k)
                dve.wait_ge(exp_s, p + 4)
                V.tensor_tensor(plo[:, r, :], p32[:, r, :], phi[:, r, :], ALU.subtract).then_inc(lo_s, 1)

            def gate_values(e, odd):
                first, second = pay[:, odd, :, 0, D + 1], pay[:, odd, :, 1, D + 1]
                dve.wait_ge(eg_s, e + 1)
                link(V.tensor_scalar(eg1[:, :], eg[:, :], 1.0, None, ALU.add))
                link(V.reciprocal(first, eg1[:, :]))
                link(V.tensor_tensor(second, eg[:, :], first, ALU.mult))

            def combine_rows(e, odd):
                link(V.tensor_tensor(ohg[:, :, :, :], oh[:, :, :, :],
                                     pay[:, odd, :, :, D + 1:ROW].to_broadcast([P, 2, 2, N_EXP]), ALU.mult))
                V.tensor_tensor(comb[:, ds(e * 2, 2), :], ohg[:, :, 0, :], ohg[:, :, 1, :], ALU.add).then_inc(cmb_s, 1)

            def route_step(e, odd, k, last_block=False):
                a = acc[odd]
                tiles = ds(e * 2, 2)
                if k == 0:
                    dve.wait_ge(pv_s, e * PAIRS + (PAIRS + 3))
                    link(V.tensor_scalar(den[:, 0, :], a[:, :, 2 * D], 0.0, 0.5, ALU.is_le, ALU.mult))
                    V.tensor_scalar(guard[:, :], den[:, 0, :], 0.5, None, ALU.add).then_inc(den_s, 1)
                    link(V.tensor_scalar(den[:, 1, :], a[:, :, 2 * D], 1e-30, 2.0, ALU.max, ALU.mult))
                    link(V.reciprocal(den[:, 0, :], den[:, 1, :]))
                if k == 2 and last_block:
                    dve.wait_ge(pstep_s, e * 4 + 2)
                    dve.wait_ge(den_s, e + 1)
                    for t in range(2):
                        last = V.scalar_tensor_tensor(g_sb[:, 2, t, :], g_sb[:, 0, t, :], guard[:, t:t + 1],
                                                      x_sb[:, 2 * e + t, :], ALU.mult, ALU.add)
                    last.then_inc(u_s, 1)
                if k == 2:
                    dve.wait_ge(u_s, e + 1)
                    for t in range(2):
                        last = V.scalar_tensor_tensor(v_sb[:, t, :], a[:, t, 0:D], den[:, 0, t:t + 1],
                                                      g_sb[:, 2, t, :], ALU.mult, ALU.add)
                    last.then_inc(v_s, 1)
                if k == 3:
                    dve.wait_ge(v_s, e + 1)
                    for t in range(2):
                        last = V.scalar_tensor_tensor(x_sb[:, ds(e * 2 + t, 1), :].rearrange("p o d -> p (o d)"),
                                                      a[:, t, D:2 * D], den[:, 0, t:t + 1],
                                                      v_sb[:, t, :], ALU.mult, ALU.add)
                    last.then_inc(accread_s, 1)
                    at_once(dve)
                    dve.wait_ge(accread_s, e + 1)
                    for t in range(2):
                        last = V.bn_stats(st2[:, t, :], x_sb[:, ds(e * 2 + t, 1), :])
                    last.then_inc(st2_s, 1)
                if k == 4:
                    at_once(dve)
                    dve.wait_ge(st2_s, e + 1)
                    for t in range(2):
                        last = V.bn_aggr(mv2[:, t, :], st2[:, t, :])
                    last.then_inc(mv_s, 1)
                if k == 6:
                    dve.wait_ge(r2_s, e + 1)
                    dve.wait_ge(pstep_s, e * 4 + 4)
                    for t in range(2):
                        last = V.tensor_scalar(pay[:, odd, t, 0, 0:D],
                                               x_sb[:, ds(e * 2 + t, 1), :],
                                               mv2[:, t, 0:1], r2[:, t:t + 1], ALU.subtract, ALU.mult)
                    last.then_inc(z_s, 1)
                if k == 9:
                    dve.wait_ge(lg_s, e + 1)
                    V.tensor_tensor(lg[:, :, :], route[:, 256:384].rearrange("p (t n) -> p t n", t=2),
                                    br[:, None, :].to_broadcast([P, 2, N_EXP]), ALU.add).then_inc(lgb_s, 1)
                    at_once(dve)
                    dve.wait_ge(lgb_s, e + 1)
                    for t in range(2):
                        last = V.max(top[:, t, :], lg[:, t, :])
                    link(last)
                    V.tensor_tensor(gap[:, :], top[:, :, 1], top[:, :, 0], ALU.subtract)
                    for t in range(2):
                        last = V.max_index(tix[:, t, :], top[:, t, :], lg[:, t, :])
                    last.then_inc(tix_s, 1)
                if k == 10:
                    dve.wait_ge(tix_s, e + 1)
                    link(V.tensor_tensor(tixf[:, :, :], tix[:, :, 0:2],
                                         padx[:, tiles][:, :, None].to_broadcast([P, 2, 2]), ALU.add))
                    link(V.tensor_tensor(oh[:, :, :, :], iota_e[:, None, None, :].to_broadcast([P, 2, 2, N_EXP]),
                                         tixf[:, :, :, None].to_broadcast([P, 2, 2, N_EXP]), ALU.is_equal))
                    V.tensor_tensor(c_all[:, odd, :, :], oh[:, :, 0, :], oh[:, :, 1, :], ALU.add).then_inc(cho_s, 1)
                if k == 11:
                    gate_values(e, odd)
                    if not last_block:
                        combine_rows(e, odd)
                if k == 12:
                    dve.wait_ge(rank_s, e + 1)
                    link(V.tensor_tensor(place[:, :, :], route[:, 384:512].rearrange("p (t n) -> p t n", t=2),
                                         region[:, None, :].to_broadcast([P, 2, N_EXP]), ALU.add))
                    dve.wait_ge(cmb_s, e if last_block else e + 1)
                    link(V.tensor_tensor(ohg[:, :, :, :], oh[:, :, :, :],
                                         place[:, :, None, :].to_broadcast([P, 2, 2, N_EXP]), ALU.mult))
                    link(V.tensor_reduce(pos[:, :, :], ohg[:, :, :, :], AX.X, ALU.add))
                    V.tensor_tensor(posi[:, odd, :, :], pos[:, :, :],
                                    padx[:, tiles][:, :, None].to_broadcast([P, 2, 2]), ALU.add).then_inc(pos_s, 1)

            def count_choices(odd):
                for t in range(2):
                    link(V.tensor_tensor(csum[:, :], csum[:, :], c_all[:, odd, t, :], ALU.add))

            def body(b, odd, routed=True, counted=True, conv=(1, 5, 7, 8)):
                for k in range(PAIRS):
                    low(b, odd, k)
                    if routed:
                        route_step(b - 1, 1 - odd, k)
                    if counted and k == 6:
                        count_choices(odd)
                    if k in conv:
                        n = conv.index(k)
                        c = convert(b * 2 + (2 + n // 2), 1 - odd, n // 2, n % 2, 2)
                        if n % 2:
                            c.then_inc(mask_s, 1)

            body(0, 0, routed=False, counted=False, conv=(5, 7, 9, 10))
            body(1, 1, counted=False)
            start = count[0]
            with dve.Fori(1, (BLOCKS - 1) // 2) as it:
                count[1] = (it - 1) * LOOP_LINKS
                for u in range(2):
                    body(it * 2 + u, u)
            assert count[0] - start == LOOP_LINKS, count[0] - start
            count[1] = 0
            count[0] = start + ((BLOCKS - 1) // 2 - 1) * LOOP_LINKS
            body(BLOCKS - 1, 0, conv=())
            for k in range(PAIRS):
                route_step(BLOCKS - 1, 0, k, last_block=True)
                if k == 6:
                    count_choices(1)

            dve.wait_ge(cnt_s, 1)
            cnt = score[0][:, 0:N_EXP]
            link(V.tensor_scalar(cnti[:, :], cnt, float(P - 1), None, ALU.add))
            V.tensor_tensor(ends[:, :], cnt, region[:, :], ALU.add)
            link(V.tensor_scalar(nti[:, :], cnti[:, :], 7, None, ALU.arith_shift_right))
            link(V.tensor_copy(ntf[:, :], nti[:, :]))
            link(V.tensor_tensor_scan(cin[:, :], ntf[:, :], zero_e[:, :], 0.0, ALU.add, ALU.add))
            V.tensor_scalar(ind2[:, :], cin[:, :], srow[:, :], None, ALU.is_gt)
            link(V.tensor_tensor(cex[:, :], cin[:, :], ntf[:, :], ALU.subtract))
            V.scalar_tensor_tensor(last_row[:, :], cex[:, :], float(P), ends[:, :], ALU.mult, ALU.add)
            link(V.scalar_tensor_tensor(ind[:, :], cex[:, :], srow[:, :], ind2[:, :], ALU.is_le, ALU.mult))
            def pick(col, values):
                return V.tensor_tensor_reduce(out=junk[:, :], in0=ind[:, :], in1=values, scale=1.0, scalar=0.0,
                                            op0=ALU.mult, op1=ALU.add, accum_out=tv[:, col:col + 1])
            link(pick(0, iota_e[:, :]))
            link(pick(2, last_row[:, :]))
            link(pick(3, ind[:, :]))
            c_ = lambda n: tv[:, n:n + 1]
            V.scalar_tensor_tensor(c_(1), c_(3), sback[:, :], c_(2), ALU.mult, ALU.add).then_inc(tv_s, 1)
            dve.wait_ge(tr_s, 1)
            V.tensor_copy(table[:, :], score[1][0:1, 0:2 * P]).then_inc(tab_s, 1)
            dve.wait_ge(pos_s, BLOCKS)
            combine_rows(BLOCKS - 1, 0)
            dve.wait_ge(tab_s, 1)
            dve.wait_ge(w1_in_s, 128)
            dve.wait_ge(w2_in_s, 7 * 16)

            def pick_w1(it, c, e):
                dve.wait_ge(hp_s, it * RING + (c + 1))
                dve.wait_ge(h0_s, it * RING + (c + 1))
                dve.wait_ge(h1_s, it * RING + (c + 1))
                V.tensor_copy(w1s[:, c % 2, :], w1_sb[:, ds(e * W1C, W1C)]).then_inc(w1s_s, 1)

            def relu(it, c):
                dve.wait_ge(hp_s, it * RING + (c + 3))
                dve.wait_ge(yp_s, it * RING + (c + 1))
                dve.wait_ge(w1s_s, it * RING + (c + 1))
                V.tensor_scalar(ht[:, c % 2, 1, :], hp[c % 2][1][:, 0:P], w1s[:, c % 2, HID + 1:HID + 2], 0.0,
                                ALU.add, ALU.max).then_inc(h1_s, 1)

            def pick_w2(it, c, e):
                if not isinstance(it, int) or it * RING + c >= 3:
                    dve.wait_ge(yp_s, it * RING + c)
                V.tensor_copy(w2s[:, c % 3, :], w2_sb[:, ds(e * HID, HID)]).then_inc(w2s_s, 1)

            expert_regs = entry_registers(dve, "expert")
            first = load_entries(dve, expert_regs, 0, 3, N_EXP - 1)
            pick_w1(0, 0, first[0])
            pick_w1(0, 1, first[1])
            pick_w2(0, 0, first[0])
            relu(0, 0)
            pick_w2(0, 1, first[1])
            pick_w1(0, 2, first[2])

            def tiles_turn(it, n):
                some = RING + 1 if n == RING else n - 2
                experts = load_entries(dve, expert_regs, it * RING + 2, some, N_EXP - 1)
                for c in range(n):
                    if n == RING or c + 1 < n:
                        relu(it + (c + 1) // RING, (c + 1) % RING)
                    if n == RING or c + 2 < n:
                        pick_w2(it + (c + 2) // RING, (c + 2) % RING, experts[c])
                    if n == RING or c + 3 < n:
                        pick_w1(it + (c + 3) // RING, (c + 3) % RING, experts[c + 1])

            expert_tiles(dve, tiles_turn)

            dve.wait_ge(hp_s, FTILES + 2)
            dve.wait_ge(w1s_s, FTILES)
            for c in range(2):
                last = V.memset(y_sb[c][96:P, TILES - 1, :], 0.0)
            last.then_inc(ypad_s, 1)
            def add_b2(h):
                t0, t1 = CHUNKS[h]
                for m in range(t0 // 2, t1 // 2):
                    dve.wait_ge(b2_s, m + 1)
                    V.tensor_tensor(x_sb[:, 2 * m:2 * m + 2, :], x_sb[:, 2 * m:2 * m + 2, :],
                                    b2p[m % 4][:, 0:2 * P].rearrange("p (t n) -> p t n", t=2), ALU.add)\
                     .then_inc(b2a_s, 1)

            def add_results(h):
                t0, t1 = CHUNKS[h]
                dve.wait_ge(b2a_s, t1 // 2)
                for c in range(2):
                    dve.wait_ge(y_in_s[h][c], 48 if t1 == TILES else 16)
                    if c == 1:
                        dve.wait_ge(half_s, h + 1)
                    V.tensor_tensor(x_sb[:, t0:t1, :], x_sb[:, t0:t1, :], y_sb[c][:, t0:t1, :], ALU.add)\
                     .then_inc(half_s if c == 0 else out_s, 1)

            add_b2(0)
            for h in range(len(CHUNKS)):
                if h + 1 < len(CHUNKS):
                    add_b2(h + 1)
                add_results(h)


def kernel(x, adj, L0_gnn_Wq, L0_gnn_Wk, L0_ffn_Wr, L0_ffn_br, L0_ffn_W1, L0_ffn_b1, L0_ffn_W2, L0_ffn_b2):
    import numpy as np
    import concourse.bacc as bacc
    from concourse import mybir as mb
    from concourse.bass_utils import run_bass_kernel_spmd

    x, adj, wq, wk, wr, br, w1, b1, w2, b2 = (np.asarray(a) for a in (
        x, adj, L0_gnn_Wq, L0_gnn_Wk, L0_ffn_Wr, L0_ffn_br, L0_ffn_W1, L0_ffn_b1, L0_ffn_W2, L0_ffn_b2))
    xp = np.zeros((NPAD, D), x.dtype)
    xp[:N_TOK] = x
    ap = np.zeros((NPAD, NPAD), adj.dtype)
    ap[:N_TOK, :N_TOK] = adj
    w1p = np.concatenate([w1.transpose(1, 0, 2), b1.reshape(N_EXP, 2, P).transpose(2, 0, 1)], axis=2)
    arrays = {
        "x_in": xp.reshape(TILES, P, D).transpose(1, 0, 2),
        "adj_in": ap,
        "wqk_in": np.concatenate([wq.T, wk.T], axis=1),
        "wr_in": wr,
        "br_in": np.broadcast_to(br[None, :], (P, N_EXP)),
        "w1_in": w1p.reshape(P, N_EXP * W1C),
        "w2_in": w2.reshape(N_EXP, 2, P, D).transpose(2, 0, 1, 3).reshape(P, N_EXP * HID),
        "b2_in": b2,
    }
    arrays = {n: np.ascontiguousarray(a) for n, a in arrays.items()}
    nc = bacc.Bacc("TRN2", target_bir_lowering=False, num_devices=1)
    args = [nc.dram_tensor(n, a.shape, mb.dt.from_np(a.dtype), kind="ExternalInput").ap() for n, a in arrays.items()]
    out = nc.dram_tensor("out", (P, TILES, D), mb.dt.float32, kind="ExternalOutput").ap()
    gnn_moe_program(nc, *args, out)
    r = run_bass_kernel_spmd(nc, [arrays], core_ids=[0])
    got = r.results[0]["out"]
    return got.transpose(1, 0, 2).reshape(NPAD, D)[:N_TOK]
```
